# Optimizing a Trainium2 kernel written in Bass

```python
import numpy as np
import jax
import jax.numpy as jnp

def _softmax(x, axis=-1):
    return jax.nn.softmax(x, axis=axis)

def _gelu(x):
    return jax.nn.gelu(x, approximate=True)

def _silu(x):
    return jax.nn.silu(x)

def _sigmoid(x):
    return jax.nn.sigmoid(x)

def _layernorm(x, axis=-1, eps=1e-05):
    m = jnp.mean(x, axis=axis, keepdims=True)
    v = jnp.var(x, axis=axis, keepdims=True)
    return (x - m) / jnp.sqrt(v + eps)

def _scatter_add(tgt, idx, src, axis=0):
    return tgt.at[idx].add(src)

def _segment_sum(src, seg, n):
    return jax.ops.segment_sum(src, seg, n)
kernel_name = 'mk_dlrm_tower_d1_rec_r8_cdc325'

def setup_inputs(seed: int=0):
    np.random.seed(seed)
    _w = jnp.asarray

    def _rec_inputs():
        import jax
        import jax.numpy as jnp
        _tk = jax.random.key(seed)
        dense_ctx = jax.random.normal(jax.random.fold_in(_tk, 190), (512, 16), jnp.float32)
        ids = jnp.stack([jax.random.randint(jax.random.fold_in(_tk, 200 + f), (512,), 0, v, jnp.int32) for f, v in enumerate([1000, 125000, 1250, 1250, 1250, 125000, 1000, 125000, 1000, 12500, 12500, 1250, 1000, 1250, 1250, 1250, 12500, 12500, 1250, 1250, 1000, 12500, 1250, 1000, 1250, 1250, 1000, 1000, 1000, 1250, 1250, 12500, 1000, 12500, 1000, 1250, 1250, 1250, 1000, 1250])], axis=1)
        tbl_0 = 0.05 * jax.random.normal(jax.random.fold_in(_tk, 500 + 0), (1000, 64), jnp.float32)
        tbl_1 = 0.05 * jax.random.normal(jax.random.fold_in(_tk, 500 + 1), (125000, 64), jnp.float32)
        tbl_2 = 0.05 * jax.random.normal(jax.random.fold_in(_tk, 500 + 2), (1250, 64), jnp.float32)
        tbl_3 = 0.05 * jax.random.normal(jax.random.fold_in(_tk, 500 + 3), (1250, 64), jnp.float32)
        tbl_4 = 0.05 * jax.random.normal(jax.random.fold_in(_tk, 500 + 4), (1250, 64), jnp.float32)
        tbl_5 = 0.05 * jax.random.normal(jax.random.fold_in(_tk, 500 + 5), (125000, 64), jnp.float32)
        tbl_6 = 0.05 * jax.random.normal(jax.random.fold_in(_tk, 500 + 6), (1000, 64), jnp.float32)
        tbl_7 = 0.05 * jax.random.normal(jax.random.fold_in(_tk, 500 + 7), (125000, 64), jnp.float32)
        tbl_8 = 0.05 * jax.random.normal(jax.random.fold_in(_tk, 500 + 8), (1000, 64), jnp.float32)
        tbl_9 = 0.05 * jax.random.normal(jax.random.fold_in(_tk, 500 + 9), (12500, 64), jnp.float32)
        tbl_10 = 0.05 * jax.random.normal(jax.random.fold_in(_tk, 500 + 10), (12500, 64), jnp.float32)
        tbl_11 = 0.05 * jax.random.normal(jax.random.fold_in(_tk, 500 + 11), (1250, 64), jnp.float32)
        tbl_12 = 0.05 * jax.random.normal(jax.random.fold_in(_tk, 500 + 12), (1000, 64), jnp.float32)
        tbl_13 = 0.05 * jax.random.normal(jax.random.fold_in(_tk, 500 + 13), (1250, 64), jnp.float32)
        tbl_14 = 0.05 * jax.random.normal(jax.random.fold_in(_tk, 500 + 14), (1250, 64), jnp.float32)
        tbl_15 = 0.05 * jax.random.normal(jax.random.fold_in(_tk, 500 + 15), (1250, 64), jnp.float32)
        tbl_16 = 0.05 * jax.random.normal(jax.random.fold_in(_tk, 500 + 16), (12500, 64), jnp.float32)
        tbl_17 = 0.05 * jax.random.normal(jax.random.fold_in(_tk, 500 + 17), (12500, 64), jnp.float32)
        tbl_18 = 0.05 * jax.random.normal(jax.random.fold_in(_tk, 500 + 18), (1250, 64), jnp.float32)
        tbl_19 = 0.05 * jax.random.normal(jax.random.fold_in(_tk, 500 + 19), (1250, 64), jnp.float32)
        tbl_20 = 0.05 * jax.random.normal(jax.random.fold_in(_tk, 500 + 20), (1000, 64), jnp.float32)
        tbl_21 = 0.05 * jax.random.normal(jax.random.fold_in(_tk, 500 + 21), (12500, 64), jnp.float32)
        tbl_22 = 0.05 * jax.random.normal(jax.random.fold_in(_tk, 500 + 22), (1250, 64), jnp.float32)
        tbl_23 = 0.05 * jax.random.normal(jax.random.fold_in(_tk, 500 + 23), (1000, 64), jnp.float32)
        tbl_24 = 0.05 * jax.random.normal(jax.random.fold_in(_tk, 500 + 24), (1250, 64), jnp.float32)
        tbl_25 = 0.05 * jax.random.normal(jax.random.fold_in(_tk, 500 + 25), (1250, 64), jnp.float32)
        tbl_26 = 0.05 * jax.random.normal(jax.random.fold_in(_tk, 500 + 26), (1000, 64), jnp.float32)
        tbl_27 = 0.05 * jax.random.normal(jax.random.fold_in(_tk, 500 + 27), (1000, 64), jnp.float32)
        tbl_28 = 0.05 * jax.random.normal(jax.random.fold_in(_tk, 500 + 28), (1000, 64), jnp.float32)
        tbl_29 = 0.05 * jax.random.normal(jax.random.fold_in(_tk, 500 + 29), (1250, 64), jnp.float32)
        tbl_30 = 0.05 * jax.random.normal(jax.random.fold_in(_tk, 500 + 30), (1250, 64), jnp.float32)
        tbl_31 = 0.05 * jax.random.normal(jax.random.fold_in(_tk, 500 + 31), (12500, 64), jnp.float32)
        tbl_32 = 0.05 * jax.random.normal(jax.random.fold_in(_tk, 500 + 32), (1000, 64), jnp.float32)
        tbl_33 = 0.05 * jax.random.normal(jax.random.fold_in(_tk, 500 + 33), (12500, 64), jnp.float32)
        tbl_34 = 0.05 * jax.random.normal(jax.random.fold_in(_tk, 500 + 34), (1000, 64), jnp.float32)
        tbl_35 = 0.05 * jax.random.normal(jax.random.fold_in(_tk, 500 + 35), (1250, 64), jnp.float32)
        tbl_36 = 0.05 * jax.random.normal(jax.random.fold_in(_tk, 500 + 36), (1250, 64), jnp.float32)
        tbl_37 = 0.05 * jax.random.normal(jax.random.fold_in(_tk, 500 + 37), (1250, 64), jnp.float32)
        tbl_38 = 0.05 * jax.random.normal(jax.random.fold_in(_tk, 500 + 38), (1000, 64), jnp.float32)
        tbl_39 = 0.05 * jax.random.normal(jax.random.fold_in(_tk, 500 + 39), (1250, 64), jnp.float32)
        _rk = jax.random.fold_in(_tk, 7)
        W_top1 = 0.0354441 * jax.random.normal(jax.random.fold_in(_tk, 801), (796, 512), jnp.float32)
        W_top2 = 0.0441942 * jax.random.normal(jax.random.fold_in(_tk, 802), (512, 256), jnp.float32)
        W_top3 = 0.0625 * jax.random.normal(jax.random.fold_in(_tk, 803), (256, 1), jnp.float32)
        b_top1 = jnp.zeros((512,), jnp.float32)
        b_top2 = jnp.zeros((256,), jnp.float32)
        return (dense_ctx, ids, tbl_0, tbl_1, tbl_2, tbl_3, tbl_4, tbl_5, tbl_6, tbl_7, tbl_8, tbl_9, tbl_10, tbl_11, tbl_12, tbl_13, tbl_14, tbl_15, tbl_16, tbl_17, tbl_18, tbl_19, tbl_20, tbl_21, tbl_22, tbl_23, tbl_24, tbl_25, tbl_26, tbl_27, tbl_28, tbl_29, tbl_30, tbl_31, tbl_32, tbl_33, tbl_34, tbl_35, tbl_36, tbl_37, tbl_38, tbl_39, W_top1, b_top1, W_top2, b_top2, W_top3)
    dense_ctx, ids, tbl_0, tbl_1, tbl_2, tbl_3, tbl_4, tbl_5, tbl_6, tbl_7, tbl_8, tbl_9, tbl_10, tbl_11, tbl_12, tbl_13, tbl_14, tbl_15, tbl_16, tbl_17, tbl_18, tbl_19, tbl_20, tbl_21, tbl_22, tbl_23, tbl_24, tbl_25, tbl_26, tbl_27, tbl_28, tbl_29, tbl_30, tbl_31, tbl_32, tbl_33, tbl_34, tbl_35, tbl_36, tbl_37, tbl_38, tbl_39, W_top1, b_top1, W_top2, b_top2, W_top3 = _rec_inputs()

    def _L0_rec_setup():
        import jax, jax.numpy as jnp
        import numpy as np
        B, N, E = (1024, 40, 64)
        P = N * (N - 1) // 2

        def _pair_indices(n):
            row, col = ([], [])
            for i in range(n - 1):
                for j in range(i + 1, n):
                    row.append(i)
                    col.append(j)
            return (np.asarray(row), np.asarray(col))
        key = jax.random.key(seed)
        k1, k2 = jax.random.split(key)
        inputs = jax.random.normal(k1, (B, N, E), dtype=jnp.float32)
        std = float(np.sqrt(2.0 / (E + E)))
        param = jax.random.normal(k2, (E, P, E), dtype=jnp.float32) * std
        return {'inputs': inputs, 'param': param}
    _L0_rec_all = _L0_rec_setup()
    _L0_rec_in = {k: v for k, v in _L0_rec_all.items() if k in ('param',)}
    del _L0_rec_all
    return {'dense_ctx': dense_ctx, 'ids': ids, 'tbl_0': tbl_0, 'tbl_1': tbl_1, 'tbl_2': tbl_2, 'tbl_3': tbl_3, 'tbl_4': tbl_4, 'tbl_5': tbl_5, 'tbl_6': tbl_6, 'tbl_7': tbl_7, 'tbl_8': tbl_8, 'tbl_9': tbl_9, 'tbl_10': tbl_10, 'tbl_11': tbl_11, 'tbl_12': tbl_12, 'tbl_13': tbl_13, 'tbl_14': tbl_14, 'tbl_15': tbl_15, 'tbl_16': tbl_16, 'tbl_17': tbl_17, 'tbl_18': tbl_18, 'tbl_19': tbl_19, 'tbl_20': tbl_20, 'tbl_21': tbl_21, 'tbl_22': tbl_22, 'tbl_23': tbl_23, 'tbl_24': tbl_24, 'tbl_25': tbl_25, 'tbl_26': tbl_26, 'tbl_27': tbl_27, 'tbl_28': tbl_28, 'tbl_29': tbl_29, 'tbl_30': tbl_30, 'tbl_31': tbl_31, 'tbl_32': tbl_32, 'tbl_33': tbl_33, 'tbl_34': tbl_34, 'tbl_35': tbl_35, 'tbl_36': tbl_36, 'tbl_37': tbl_37, 'tbl_38': tbl_38, 'tbl_39': tbl_39, 'W_top1': W_top1, 'b_top1': b_top1, 'W_top2': W_top2, 'b_top2': b_top2, 'W_top3': W_top3, 'L0_rec_param': _L0_rec_in['param']}

def reference(dense_ctx, ids, tbl_0, tbl_1, tbl_2, tbl_3, tbl_4, tbl_5, tbl_6, tbl_7, tbl_8, tbl_9, tbl_10, tbl_11, tbl_12, tbl_13, tbl_14, tbl_15, tbl_16, tbl_17, tbl_18, tbl_19, tbl_20, tbl_21, tbl_22, tbl_23, tbl_24, tbl_25, tbl_26, tbl_27, tbl_28, tbl_29, tbl_30, tbl_31, tbl_32, tbl_33, tbl_34, tbl_35, tbl_36, tbl_37, tbl_38, tbl_39, W_top1, b_top1, W_top2, b_top2, W_top3, L0_rec_param):
    import jax
    import jax.numpy as jnp

    def _L0_rec_ref(inputs, param):
        import jax, jax.numpy as jnp
        import numpy as np
        B, N, E = (1024, 40, 64)
        P = N * (N - 1) // 2

        def _pair_indices(n):
            row, col = ([], [])
            for i in range(n - 1):
                for j in range(i + 1, n):
                    row.append(i)
                    col.append(j)
            return (np.asarray(row), np.asarray(col))
        n = inputs.shape[1]
        rowidx, colidx = _pair_indices(n)
        p = inputs[:, rowidx]
        q = inputs[:, colidx]
        out = jnp.einsum('bie,fie,bif->bi', p, param, q)
        return out[:, None, :]
    e = jnp.stack([tbl_0[ids[:, 0]], tbl_1[ids[:, 1]], tbl_2[ids[:, 2]], tbl_3[ids[:, 3]], tbl_4[ids[:, 4]], tbl_5[ids[:, 5]], tbl_6[ids[:, 6]], tbl_7[ids[:, 7]], tbl_8[ids[:, 8]], tbl_9[ids[:, 9]], tbl_10[ids[:, 10]], tbl_11[ids[:, 11]], tbl_12[ids[:, 12]], tbl_13[ids[:, 13]], tbl_14[ids[:, 14]], tbl_15[ids[:, 15]], tbl_16[ids[:, 16]], tbl_17[ids[:, 17]], tbl_18[ids[:, 18]], tbl_19[ids[:, 19]], tbl_20[ids[:, 20]], tbl_21[ids[:, 21]], tbl_22[ids[:, 22]], tbl_23[ids[:, 23]], tbl_24[ids[:, 24]], tbl_25[ids[:, 25]], tbl_26[ids[:, 26]], tbl_27[ids[:, 27]], tbl_28[ids[:, 28]], tbl_29[ids[:, 29]], tbl_30[ids[:, 30]], tbl_31[ids[:, 31]], tbl_32[ids[:, 32]], tbl_33[ids[:, 33]], tbl_34[ids[:, 34]], tbl_35[ids[:, 35]], tbl_36[ids[:, 36]], tbl_37[ids[:, 37]], tbl_38[ids[:, 38]], tbl_39[ids[:, 39]]], axis=1)
    z = _L0_rec_ref(e, L0_rec_param)
    z = z.reshape(z.shape[0], -1)
    h = jnp.concatenate([z, dense_ctx], axis=1)
    h = jnp.maximum(h @ W_top1 + b_top1, 0.0)
    h = jnp.maximum(h @ W_top2 + b_top2, 0.0)
    y = h @ W_top3
    return y

_drawn_inputs = setup_inputs


def setup_inputs(seed=0):
    import zlib

    import numpy as np

    out = dict(_drawn_inputs(seed))
    spreads = {'b_top1': (0.0, 0.1), 'b_top2': (0.0, 0.1)}
    factors = {}
    for name, (base, spread) in spreads.items():
        noise = np.random.default_rng([zlib.crc32(name.encode()), seed]).standard_normal(out[name].shape)
        drawn = base * np.exp(spread * noise) if base else spread * noise
        out[name] = jnp.asarray(drawn.astype(out[name].dtype))
    for name, factor in factors.items():
        out[name] = (out[name] * factor).astype(out[name].dtype)
    return out
```

```python
import numpy as np
import concourse.bass as bass
from concourse import mybir

BATCH, FIELDS, EMB, DENSE = 512, 40, 64, 16
H1, H2 = 512, 256
P = 128
BT = BATCH // P
PAIRS = FIELDS * (FIELDS - 1) // 2

TILES = []
for _k in range(1, FIELDS):
    _ms = list(range((_k + 1) // 2))
    TILES += [(_k, m) for m in (_ms if _k % 2 else _ms[::-1])]
NT = len(TILES)
FIRST_TILE = {k: min(t for t, x in enumerate(TILES) if x[0] == k) for k in range(1, FIELDS)}
LAST_TILE = {k: max(t for t, x in enumerate(TILES) if x[0] == k) for k in range(1, FIELDS)}
SLOTS = NT // 2
QUADS = NT // 4
CHUNK = 16
CHUNKS = NT // CHUNK
ZT = 64
ZB = -(-NT // ZT)
Z_WINDOWS = ZT // 4
DENSE_ROW = 2 * ((NT % ZT) // 4)


def pair_index(i, j):
    return i * (2 * FIELDS - i - 1) // 2 + j - i - 1


def z_row(t, half):
    return P * (t // ZT) + 32 * (t % 4) + 2 * ((t % ZT) // 4) + half


def place_in_slot(t):
    a, b = TILES[t - t % 2][1], TILES[t - t % 2 + 1][1]
    return t % 2 if a <= b else 1 - t % 2


RAW_RING, LO_RING, STACK_RING = 3, 2, 5
G_RING, K_RING, U_RING, PROD_RING = 6, 3, 3, 4
AHEAD = 3
LO_ON_VECTOR = 3


def schedule():
    steps = [("T", 0), ("T", 1)]
    transposed = 2
    for s in range(SLOTS):
        t = 2 * s
        while transposed < FIELDS:
            k = transposed
            lead = 2 if k < 13 else 6
            if t + 1 >= FIRST_TILE[k] - lead and t >= FIRST_TILE[max(k - 1, 1)] - 1 or t + 1 >= FIRST_TILE[k]:
                steps.append(("T", k))
                transposed += 1
            else:
                break
        steps.append(("M", s))
        if s % 2 and s >= 3:
            steps.append(("S", s // 2 - 1))
    return steps


def pool_order():
    order, c = [], LO_ON_VECTOR
    for k in range(FIELDS):
        order.append(("gather", k))
        while c < CHUNKS and k >= TILES[CHUNK * (c - 2)][0] + 2:
            order.append(("lo", c))
            c += 1
    return order + [("lo", x) for x in range(c, CHUNKS)]


def build(nc, tables, ids, param, ident, sel, dense_sel, dense, w1, b1, w2, b2, w3, out):
    f32, f32r, i32 = mybir.dt.float32, mybir.dt.float32r, mybir.dt.int32
    ALU = mybir.AluOpType
    ACT = mybir.ActivationFunctionType
    STEPS = schedule()
    from contextlib import ExitStack
    ctx = ExitStack()
    with ctx:
        def sb(name, shape, dt=f32):
            return ctx.enter_context(nc.sbuf_tensor(name, shape, dt))

        def sem(name):
            return ctx.enter_context(nc.semaphore(name))

        ids_sb = sb("ids_sb", [P, BT, FIELDS], i32)
        ident_sb = sb("ident_sb", [P, P])
        sel_sb = sb("sel_sb", [P, 62])
        dsel_sb = sb("dsel_sb", [DENSE, 32])
        dense_sb = sb("dense_sb", [DENSE, BATCH])
        gathered = sb("gathered", [P, G_RING, BT, EMB])
        twice = sb("twice", [P, 2, BT, 2, EMB])
        e_pairs = sb("e_pairs", [P, FIELDS // 2, BATCH])
        e_hi = sb("e_hi", [P, K_RING, BATCH], f32r)
        e_lo = sb("e_lo", [P, K_RING, BATCH], f32r)
        raw = sb("raw", [P, RAW_RING, CHUNK // 2 * P])
        hi = sb("hi", [P, RAW_RING, CHUNK // 2 * P], f32r)
        lo = sb("lo", [P, LO_RING, CHUNK // 2 * P], f32r)
        stack = sb("stack", [P, STACK_RING, 2, CHUNK // 2 * P], f32r)
        prod = sb("prod", [P, PROD_RING, 2, BATCH])
        z_sb = sb("z_sb", [P, ZB, BATCH])
        w1_sb = sb("w1_sb", [P, ZB, H1])
        w2_sb = sb("w2_sb", [P, H1 // P, H2])
        w3_sb = sb("w3_sb", [P, H2 // P, 1])
        b1_sb = sb("b1_sb", [P, H1 // P])
        b2_sb = sb("b2_sb", [P, H2 // P])
        h1_sb = sb("h1_sb", [P, H1 // P, BATCH])
        h2_sb = sb("h2_sb", [P, H2 // P, BATCH])
        y_sb = sb("y_sb", [1, BATCH])

        psum = ctx.enter_context(nc.psum_tensor("psum", [P, 8, BATCH], f32))
        Z_BANK, T_BANK = 6, 7

        ids_in, const_in, mlp_in = sem("ids_in"), sem("const_in"), sem("mlp_in")
        raw_in = [sem(f"raw_in{i}") for i in range(RAW_RING)]
        lo_in = [sem(f"lo_in{i}") for i in range(STACK_RING)]
        field_in = [sem(f"field_in{i}") for i in range(G_RING)]
        hi_done = sem("hi_done")
        hi_stacked = sem("hi_stacked")
        lo_dve, lo_pool = sem("lo_dve"), sem("lo_pool")
        doubled = sem("doubled")
        transposed = sem("transposed")
        e_pair_done = sem("e_pair_done")
        e_lo_done = sem("e_lo_done")
        u_done = sem("u_done")
        prod_done = sem("prod_done")
        reduced = sem("reduced")
        z_done = sem("z_done")
        h1_mm, h1_act, h1_dve = sem("h1_mm"), sem("h1_act"), sem("h1_dve")
        h2_mm, h2_act, h2_dve = sem("h2_mm"), sem("h2_act"), sem("h2_dve")
        y_mm, y_done, stored = sem("y_mm"), sem("y_done"), sem("stored")
        block = ctx.enter_context(nc.Block())

        def lo_ready(eng, c):
            if c < LO_ON_VECTOR:
                eng.wait_ge(lo_dve, c + 1)
            else:
                eng.wait_ge(lo_pool, c + 1 - LO_ON_VECTOR)

        def moved_out(eng, c):
            if c >= LO_RING:
                b = c - LO_RING
                eng.wait_ge(lo_in[b % STACK_RING], 32 * (b // STACK_RING + 1))

        def slots_of_field(k):
            return LAST_TILE[k] // 2 + 1

        @block.sync
        def _(sp):
            sp.dma_start(ids_sb[:], ids).then_inc(ids_in, 16)

            def load(c):
                if c >= RAW_RING:
                    sp.wait_ge(hi_stacked, c - RAW_RING + 1)
                    lo_ready(sp, c - RAW_RING)
                sp.dma_start(raw[:, c % RAW_RING, :], param[c]).then_inc(raw_in[c % RAW_RING], 16)

            load(0)
            sp.dma_start(ident_sb[:], ident).then_inc(const_in, 16)
            sp.dma_start(sel_sb[:], sel).then_inc(const_in, 16)
            for c in range(1, RAW_RING):
                load(c)
            for c in range(CHUNKS):
                lo_ready(sp, c)
                if c >= STACK_RING:
                    sp.wait_ge(u_done, (c - STACK_RING + 1) * CHUNK // 2)
                for half in range(2):
                    sp.dma_start(stack[P // 2 * (1 - half):P // 2 * (2 - half), c % STACK_RING, half, :].bitcast(f32),
                                 lo[P // 2 * half:P // 2 * (half + 1), c % LO_RING, :].bitcast(f32))\
                      .then_inc(lo_in[c % STACK_RING], 16)
                if c + RAW_RING < CHUNKS:
                    load(c + RAW_RING)
                if c == 4:
                    sp.dma_start(dsel_sb[:], dense_sel).then_inc(mlp_in, 16)
                    sp.dma_start(dense_sb[:], dense).then_inc(mlp_in, 16)
                    sp.dma_start(w1_sb[:], w1).then_inc(mlp_in, 16)
                    sp.dma_start(b1_sb[:], b1).then_inc(mlp_in, 16)
                    sp.dma_start(w2_sb[:], w2).then_inc(mlp_in, 16)
                    sp.dma_start(b2_sb[:], b2).then_inc(mlp_in, 16)
                    sp.dma_start(w3_sb[:], w3).then_inc(mlp_in, 16)
            sp.wait_ge(y_done, 1)
            sp.dma_start(out, y_sb[:]).then_inc(stored, 16)
            sp.wait_ge(stored, 16)

        @block.gpsimd
        def _(pool):
            pool.wait_ge(ids_in, 16)
            for what, n in pool_order():
                if what == "gather":
                    if n >= G_RING:
                        pool.wait_ge(doubled, n - G_RING + 1)
                    for bt in range(BT):
                        pool.indirect_dma_start(
                            out=gathered[:, n % G_RING, bt, :], out_offset=None, in_=tables[n],
                            in_offset=bass.IndirectOffsetOnAxis(ap=ids_sb[:, bt, n:n + 1], axis=0))\
                            .then_inc(field_in[n % G_RING], 16)
                else:
                    pool.wait_ge(hi_done, n + 1)
                    moved_out(pool, n)
                    nc.gpsimd.tensor_tensor(lo[:, n % LO_RING, :], raw[:, n % RAW_RING, :],
                                            hi[:, n % RAW_RING, :].bitcast(f32), ALU.subtract)\
                      .then_inc(lo_pool, 1)

        @block.scalar
        def _(act):
            def split(c):
                act.wait_ge(raw_in[c % RAW_RING], 16 * (c // RAW_RING + 1))
                if c >= RAW_RING:
                    lo_ready(act, c - RAW_RING)
                nc.scalar.copy(hi[:, c % RAW_RING, :], raw[:, c % RAW_RING, :]).then_inc(hi_done, 1)
                if c >= STACK_RING:
                    act.wait_ge(u_done, (c - STACK_RING + 1) * CHUNK // 2)
                for half in range(2):
                    rows = slice(P // 2 * half, P // 2 * (half + 1))
                    last = nc.scalar.copy(stack[rows, c % STACK_RING, half, :], raw[rows, c % RAW_RING, :])
                last.then_inc(hi_stacked, 1)

            for c in range(AHEAD):
                split(c)
            for what, n in STEPS:
                if what == "T":
                    act.wait_ge(field_in[n % G_RING], 16 * BT * (n // G_RING + 1))
                    if n >= 2:
                        act.wait_ge(transposed, n - 1)
                    nc.scalar.copy(twice[:, n % 2, :, :, :], gathered[:, n % G_RING, :, :].rearrange(
                        "p t (o e) -> p t o e", o=1).to_broadcast([P, BT, 2, EMB])).then_inc(doubled, 1)
                    act.wait_ge(transposed, n + 1)
                    if n >= K_RING + 1:
                        act.wait_ge(u_done, slots_of_field(n - K_RING))
                    nc.scalar.copy(e_hi[:, n % K_RING, :], psum[:, T_BANK, :])
                    rows = slice(EMB * (n % 2), EMB * (n % 2 + 1))
                    nc.scalar.copy(e_pairs[rows, n // 2, :], psum[rows, T_BANK, :]).then_inc(e_pair_done, 1)
                elif what == "M" and n % (CHUNK // 2) == 0 and n // (CHUNK // 2) + AHEAD < CHUNKS:
                    split(n // (CHUNK // 2) + AHEAD)
                elif what == "S" and (n + 1) % Z_WINDOWS == 0:
                    act.wait_ge(reduced, n + 1)
                    nc.scalar.copy(z_sb[:, n // Z_WINDOWS, :], psum[:, Z_BANK, :]).then_inc(z_done, 1)
            act.wait_ge(reduced, QUADS + 1)
            nc.scalar.copy(z_sb[:, ZB - 1, :], psum[:, Z_BANK, :]).then_inc(z_done, 1)
            act.wait_ge(mlp_in, 7 * 16)
            for n in range(0, H1 // P, 2):
                act.wait_ge(h1_mm, n + 1)
                nc.scalar.activation(h1_sb[:, n, :], psum[:, n, :], ACT.Relu, bias=b1_sb[:, n:n + 1])\
                  .then_inc(h1_act, 1)
            act.wait_ge(h2_mm, 1)
            nc.scalar.activation(h2_sb[:, 0, :], psum[:, 4, :], ACT.Relu, bias=b2_sb[:, 0:1]).then_inc(h2_act, 1)
            act.wait_ge(y_mm, 1)
            nc.scalar.copy(y_sb[:], psum[0:1, 6, :]).then_inc(y_done, 1)

        @block.vector
        def _(dve):
            for c in range(LO_ON_VECTOR):
                dve.wait_ge(hi_done, c + 1)
                moved_out(dve, c)
                nc.vector.tensor_tensor(lo[:, c % LO_RING, :], raw[:, c % RAW_RING, :],
                                        hi[:, c % RAW_RING, :].bitcast(f32), ALU.subtract).then_inc(lo_dve, 1)
            for what, n in STEPS:
                if what == "T":
                    dve.wait_ge(e_pair_done, n + 1)
                    nc.vector.tensor_tensor(e_lo[:, n % K_RING, :], psum[:, T_BANK, :],
                                            e_hi[:, n % K_RING, :].bitcast(f32), ALU.subtract)\
                      .then_inc(e_lo_done, 1)
                elif what == "M":
                    dve.wait_ge(u_done, n + 1)
                    dve.wait_ge(e_pair_done, TILES[2 * n + 1][0] + 1)
                    if n >= PROD_RING:
                        dve.wait_ge(reduced, (n - PROD_RING) // 2 + 1)
                    m = sorted((TILES[2 * n][1], TILES[2 * n + 1][1]))
                    if m[0] == m[1]:
                        e = e_pairs[:, m[0]:m[0] + 1, :].to_broadcast([P, 2, BATCH])
                    else:
                        e = e_pairs[:, m[0]:m[1] + 1, :]
                    u = 2 * (n % U_RING)
                    nc.vector.tensor_tensor(prod[:, n % PROD_RING, :, :], psum[:, u:u + 2, :], e, ALU.mult)\
                      .then_inc(prod_done, 1)
            dve.wait_ge(mlp_in, 7 * 16)
            for n in range(1, H1 // P, 2):
                dve.wait_ge(h1_mm, n + 1)
                nc.vector.tensor_scalar(h1_sb[:, n, :], psum[:, n, :], b1_sb[:, n:n + 1], 0.0, ALU.add, ALU.max)\
                  .then_inc(h1_dve, 1)
            dve.wait_ge(h2_mm, 2)
            nc.vector.tensor_scalar(h2_sb[:, 1, :], psum[:, 5, :], b2_sb[:, 1:2], 0.0, ALU.add, ALU.max)\
              .then_inc(h2_dve, 1)

        @block.tensor
        def _(pe):
            pe.wait_ge(const_in, 32)

            def transpose_field(k):
                pe.wait_ge(doubled, k + 1)
                if k:
                    pe.wait_ge(e_lo_done, k)
                for bt in range(BT):
                    last = nc.tensor.transpose(psum[:, T_BANK, P * bt:P * (bt + 1)],
                                               twice[:, k % 2, bt, :, :].rearrange("p o e -> p (o e)"), ident_sb[:])
                last.then_inc(transposed, 1)

            def multiply_slot(s):
                if s >= U_RING:
                    pe.wait_ge(prod_done, s - U_RING + 1)
                for t in (2 * s, 2 * s + 1):
                    k = TILES[t][0]
                    c, u = t // CHUNK, t % CHUNK // 2
                    if t % CHUNK == 0:
                        pe.wait_ge(hi_stacked, c + 1)
                        pe.wait_ge(lo_in[c % STACK_RING], 32 * (c // STACK_RING + 1))
                    if t == FIRST_TILE[k]:
                        pe.wait_ge(e_lo_done, k + 1)
                    weights = stack[:, c % STACK_RING, t % 2, P * u:P * (u + 1)]
                    bank = psum[:, 2 * (s % U_RING) + place_in_slot(t), :]
                    nc.tensor.matmul(bank, weights, e_hi[:, k % K_RING, :], start=True, stop=False)
                    last = nc.tensor.matmul(bank, weights, e_lo[:, k % K_RING, :], start=False, stop=True)
                last.then_inc(u_done, 1)

            def reduce_quad(q):
                w = q % Z_WINDOWS
                pe.wait_ge(prod_done, 2 * q + 2)
                if q and w == 0:
                    pe.wait_ge(z_done, q // Z_WINDOWS)
                last_window = Z_WINDOWS - 1 if q < QUADS - QUADS % Z_WINDOWS else QUADS % Z_WINDOWS - 1
                for g in range(4):
                    t = 4 * q + g
                    last = nc.tensor.matmul(psum[32 * g:32 * g + 32, Z_BANK, :], sel_sb[:, 30 - 2 * w:62 - 2 * w],
                                            prod[:, (t // 2) % PROD_RING, place_in_slot(t), :],
                                            start=(w == 0), stop=(w == last_window and (g > 0 or q < QUADS - 1)),
                                            skip_group_check=True)
                last.then_inc(reduced, 1)

            for what, n in STEPS:
                {"T": transpose_field, "M": multiply_slot, "S": reduce_quad}[what](n)

            def layer1(b, last_block):
                for n in range(H1 // P):
                    mm = nc.tensor.matmul(psum[:, n, :], w1_sb[:, b, P * n:P * (n + 1)], z_sb[:, b, :],
                                          start=(b == 0), stop=last_block)
                    if last_block:
                        mm.then_inc(h1_mm, 1)

            pe.wait_ge(mlp_in, 7 * 16)
            pe.wait_ge(prod_done, SLOTS)
            reduce_quad(QUADS - 1)
            nc.tensor.matmul(psum[0:32, Z_BANK, :], dsel_sb[:], dense_sb[:], start=False, stop=True,
                             skip_group_check=True).then_inc(reduced, 1)
            for b in range(ZB):
                pe.wait_ge(z_done, b + 1)
                layer1(b, b == ZB - 1)
            for c in range(H1 // P):
                pe.wait_ge(h1_dve if c % 2 else h1_act, c // 2 + 1)
                for n in range(H2 // P):
                    mm = nc.tensor.matmul(psum[:, 4 + n, :], w2_sb[:, c, P * n:P * (n + 1)], h1_sb[:, c, :],
                                          start=(c == 0), stop=(c == H1 // P - 1))
                    if c == H1 // P - 1:
                        mm.then_inc(h2_mm, 1)
            for c in range(H2 // P):
                pe.wait_ge(h2_dve if c else h2_act, 1)
                mm = nc.tensor.matmul(psum[0:1, 6, :], w3_sb[:, c, :], h2_sb[:, c, :],
                                      start=(c == 0), stop=(c == H2 // P - 1))
            mm.then_inc(y_mm, 1)


def kernel(**inputs):
    import concourse.bacc as bacc
    from concourse.bass_utils import run_bass_kernel_spmd

    x = {k: np.asarray(v) for k, v in inputs.items()}

    pairs = np.array([[pair_index(2 * m + h, k) if 2 * m + h < k else PAIRS for h in range(2)] for k, m in TILES])
    param = x["L0_rec_param"]
    param = np.concatenate([param, np.zeros((EMB, 1, EMB), param.dtype)], axis=1)[:, pairs.reshape(-1), :]
    param = param.reshape(EMB, CHUNKS, CHUNK // 2, 2, P).transpose(1, 3, 0, 2, 4).reshape(CHUNKS, P, CHUNK // 2 * P)

    rows = np.full(ZB * P, PAIRS + DENSE)
    for t in range(NT):
        for h in range(2):
            if pairs[t, h] < PAIRS:
                rows[z_row(t, h)] = pairs[t, h]
    rows[(ZB - 1) * P + DENSE_ROW:(ZB - 1) * P + DENSE_ROW + DENSE] = PAIRS + np.arange(DENSE)
    w1 = x["W_top1"]
    w1 = np.concatenate([w1, np.zeros((1, H1), w1.dtype)])[rows].reshape(ZB, P, H1).transpose(1, 0, 2)

    sel = np.zeros((P, 62), np.float32)
    sel[:EMB, 30] = 1
    sel[EMB:, 31] = 1
    dense_sel = np.zeros((DENSE, 32), np.float32)
    dense_sel[np.arange(DENSE), DENSE_ROW + np.arange(DENSE)] = 1

    arrays = {f"tbl{k}": x[f"tbl_{k}"] for k in range(FIELDS)}
    arrays |= {
        "idx": x["ids"].reshape(BT, P, FIELDS).transpose(1, 0, 2),
        "param": param, "ident": np.eye(P, dtype=np.float32), "sel": sel, "dense_sel": dense_sel,
        "dense": x["dense_ctx"].T, "w1": w1, "b1": x["b_top1"].reshape(H1 // P, P).T,
        "w2": x["W_top2"].reshape(H1 // P, P, H2).transpose(1, 0, 2), "b2": x["b_top2"].reshape(H2 // P, P).T,
        "w3": x["W_top3"].reshape(H2 // P, P, 1).transpose(1, 0, 2),
    }
    arrays = {f"in_{n}": np.ascontiguousarray(a) for n, a in arrays.items()}
    nc = bacc.Bacc("TRN2", target_bir_lowering=False, num_devices=1)
    ap = {n: nc.dram_tensor(n, a.shape, mybir.dt.from_np(a.dtype), kind="ExternalInput").ap() for n, a in arrays.items()}
    y = nc.dram_tensor("out_y", (1, BATCH), mybir.dt.float32, kind="ExternalOutput").ap()
    build(nc, [ap[f"in_tbl{k}"] for k in range(FIELDS)],
          *(ap[f"in_{n}"] for n in ("idx", "param", "ident", "sel", "dense_sel", "dense", "w1", "b1", "w2", "b2", "w3")), y)
    result = run_bass_kernel_spmd(nc, [arrays], core_ids=[0])
    return result.results[0]["out_y"].reshape(BATCH, 1)
```

```python
import numpy as np
import concourse.bass as bass
from concourse import mybir

BATCH, FIELDS, EMB, DENSE = 512, 40, 64, 16
H1, H2 = 512, 256
P = 128
BT = BATCH // P
PAIRS = FIELDS * (FIELDS - 1) // 2

SMALL = (0, 6)
VOCAB = 1000
VT = 8
VR = VOCAB // VT
ORDER = [*SMALL, *(f for f in range(FIELDS) if f not in SMALL)]


def is_small(k):
    return ORDER[k] in SMALL


def smalls(k):
    return sum(is_small(x) for x in range(k + 1))


def gathers(k):
    return k + 1 - smalls(k)


TILES = []
for _k in range(1, FIELDS):
    _ms = list(range((_k + 1) // 2))
    TILES += [(_k, m) for m in (_ms if _k % 2 else _ms[::-1])]
NT = len(TILES)
FIRST_TILE = {k: min(t for t, x in enumerate(TILES) if x[0] == k) for k in range(1, FIELDS)}
LAST_TILE = {k: max(t for t, x in enumerate(TILES) if x[0] == k) for k in range(1, FIELDS)}
SLOTS = NT // 2
QUADS = NT // 4
CHUNK = 16
CHUNKS = NT // CHUNK
ZT = 64
ZB = -(-NT // ZT)
W1_CHUNKS = -(-ZB // 2)
ALL_CHUNKS = CHUNKS + W1_CHUNKS
Z_WINDOWS = ZT // 4
DENSE_ROW = 2 * ((NT % ZT) // 4)


SMALL_AT = [k for k in range(FIELDS) if is_small(k)]
GATHERED_AT = [k for k in range(FIELDS) if not is_small(k)]


def pair_index(i, j):
    return i * (2 * FIELDS - i - 1) // 2 + j - i - 1


def z_row(t, half):
    return P * (t // ZT) + 32 * (t % 4) + 2 * ((t % ZT) // 4) + half


def place_in_slot(t):
    a, b = TILES[t - t % 2][1], TILES[t - t % 2 + 1][1]
    return t % 2 if a <= b else 1 - t % 2


Z_BANK, E_BANKS = 6, (7, 4)
EARLY_SLOTS, EARLY_FIELDS = 12, 9


def slot_bank(s):
    return 2 * (s % 2) if s < EARLY_SLOTS else 2 * (s % 3)


def field_bank(k):
    return E_BANKS[k % 2] if k < EARLY_FIELDS else E_BANKS[0]


def last_with(bank_of, n, bank):
    return max((x for x in range(n) if bank_of(x) == bank), default=None)


RAW_RING, HI_RING, LO_RING, STACK_RING = 3, 2, 2, 5
G_RING, D_RING, K_RING, PROD_RING = 6, 3, 5, 4
AHEAD = 3
LO_ON_VECTOR = 6
FIRST_CHUNKS = {0: 0, 1: 2, 2: 4, 3: 7}


DOUBLED_AHEAD, LO_LATER = 1, 2
ONEHOT_AHEAD = 1


def lead(k):
    return 1 if k < 6 else 3 if k < 10 else 5


def schedule():
    steps, later = [], []

    def add(step, *followers):
        steps.append(step)
        if step[0] in "MT":
            for x in later:
                x[0] -= 1
            while any(x[0] <= 0 for x in later):
                x = next(x for x in later if x[0] <= 0)
                later.remove(x)
                steps.append(x[1])
        later.extend([n, x] for n, x in followers)

    def chunk(c, gap):
        lo_part = [(LO_LATER, ("L", c))] if c < LO_ON_VECTOR else []
        halves = [(gap, ("H", 2 * c)), (2 * gap, ("H", 2 * c + 1))] if c < CHUNKS else []
        add(("W", c), *lo_part, *halves)

    k = 0
    for s in range(SLOTS):
        while k < FIELDS and (k < 2 or 2 * s + 1 >= FIRST_TILE[k] - lead(k)):
            for x in range(len(SMALL)):
                if max(x - ONEHOT_AHEAD, 0) == k:
                    add(("O", x))
            for c, before in FIRST_CHUNKS.items():
                if before == k:
                    chunk(c, 1)
            for x in range(FIELDS):
                if not is_small(x) and max(x - DOUBLED_AHEAD, 0) == k:
                    add(("D", x))
            add(("T", k), (1, ("P", k)))
            k += 1
        if s and 2 * s % CHUNK == 0:
            chunk(2 * s // CHUNK + AHEAD, 1)
        add(("M", s))
        if s % 2 and s >= 3:
            steps.append(("S", s // 2 - 1))
    return steps + [("W", c) for c in range(CHUNKS + AHEAD, ALL_CHUNKS)] + [("S", QUADS - 1)]


def pool_order():
    order, c = [], LO_ON_VECTOR
    for k in range(FIELDS):
        if not is_small(k):
            order.append(("gather", k))
        while c < CHUNKS and k >= TILES[CHUNK * (c - AHEAD)][0] + 3:
            order.append(("lo", c))
            c += 1
    return order + [("lo", x) for x in range(c, ALL_CHUNKS)]


def build(nc, tables, ids, ids_row, row_no, chunks, ident, sel, dense_sel, dense, b1, w2, b2, w3, out):
    f32, f32r, i32 = mybir.dt.float32, mybir.dt.float32r, mybir.dt.int32
    ALU = mybir.AluOpType
    ACT = mybir.ActivationFunctionType
    STEPS = schedule()
    from contextlib import ExitStack
    ctx = ExitStack()
    with ctx:
        def sb(name, shape, dt=f32):
            return ctx.enter_context(nc.sbuf_tensor(name, shape, dt))

        def sem(name):
            return ctx.enter_context(nc.semaphore(name))

        row_no_sb = sb("row_no_sb", [P, VT])
        ids_sb = sb("ids_sb", [P, BT, FIELDS], i32)
        ident_sb = sb("ident_sb", [P, P])
        sel_sb = sb("sel_sb", [P, 62])
        dsel_sb = sb("dsel_sb", [DENSE, 32])
        dense_sb = sb("dense_sb", [DENSE, BATCH])
        gathered = sb("gathered", [P, G_RING, BT, EMB])
        twice = sb("twice", [P, D_RING, BT, 2, EMB])
        e_pairs = sb("e_pairs", [P, FIELDS // 2, BATCH])
        e_hi = sb("e_hi", [P, K_RING, BATCH], f32r)
        e_lo = sb("e_lo", [P, K_RING, BATCH], f32r)
        raw = sb("raw", [P, RAW_RING, CHUNK // 2 * P])
        hi = sb("hi", [P, HI_RING, CHUNK // 2 * P], f32r)
        lo = sb("lo", [P, LO_RING, CHUNK // 2 * P], f32r)
        stack = sb("stack", [P, STACK_RING, 2, CHUNK // 2 * P], f32r)
        prod = sb("prod", [P, PROD_RING, 2, BATCH])
        table_parts = [sb(f"table_parts{i}", [VR, VT, 2 * EMB], f32r) for i in range(2)]
        z_parts = sb("z_parts", [P, 2 * ZB, BATCH], f32r)
        z_hi, z_lo = z_parts[:, 0:ZB, :], z_parts[:, ZB:2 * ZB, :]
        w2_sb = sb("w2_sb", [P, H1 // P, H2])
        w3_sb = sb("w3_sb", [P, H2 // P, 1])
        b1_sb = sb("b1_sb", [P, H1 // P])
        b2_sb = sb("b2_sb", [P, H2 // P])
        h1_sb, h2_sb, y_sb = e_pairs[:, 0:4, :], e_pairs[:, 4:6, :], e_pairs[0:1, 6, :]
        onehot = z_parts[0:VR, :, :]
        ids_all = [e_pairs[0:VR, 16 + i, :].bitcast(i32) for i in range(2)]
        table_raw = [e_pairs[0:VR, 18 + i, :].rearrange("p (c x) -> p c x", x=EMB) for i in range(2)]

        psum = ctx.enter_context(nc.psum_tensor("psum", [P, 8, BATCH], f32))
        MLP_LOADS = 6

        ids_in, row_no_in, const_in, mlp_in = sem("ids_in"), sem("row_no_in"), sem("const_in"), sem("mlp_in")
        raw_in = [sem(f"raw_in{i}") for i in range(RAW_RING)]
        lo_in = [sem(f"lo_in{i}") for i in range(STACK_RING)]
        field_in = [sem(f"field_in{i}") for i in range(G_RING)]
        hi_done = sem("hi_done")
        hi_stacked = sem("hi_stacked")
        lo_dve, lo_pool = sem("lo_dve"), sem("lo_pool")
        small_in = [sem(f"small_in{i}") for i in range(2)]
        table_hi, table_lo = sem("table_hi"), sem("table_lo")
        onehot_done = sem("onehot_done")
        parts_done, small_pair_done = sem("parts_done"), sem("small_pair_done")
        doubled = sem("doubled")
        transposed = sem("transposed")
        e_hi_done, e_pair_done = sem("e_hi_done"), sem("e_pair_done")
        e_lo_done = sem("e_lo_done")
        u_done = sem("u_done")
        prod_done = sem("prod_done")
        reduced = sem("reduced")
        z_hi_done, z_lo_done = sem("z_hi_done"), sem("z_lo_done")
        h1_mm, h1_act, h1_dve = sem("h1_mm"), sem("h1_act"), sem("h1_dve")
        h2_mm, h2_act, h2_dve = sem("h2_mm"), sem("h2_act"), sem("h2_dve")
        y_mm, y_done, stored = sem("y_mm"), sem("y_done"), sem("stored")
        block = ctx.enter_context(nc.Block())

        def lo_ready(eng, c):
            if c < LO_ON_VECTOR:
                eng.wait_ge(lo_dve, c + 1)
            else:
                eng.wait_ge(lo_pool, c + 1 - LO_ON_VECTOR)

        def moved_out(eng, c):
            if c >= LO_RING:
                b = c - LO_RING
                eng.wait_ge(lo_in[b % STACK_RING], 32 * (b // STACK_RING + 1))

        def block_ends(q):
            return (q + 1) % Z_WINDOWS == 0 or q == QUADS - 1

        def parts_ready(eng, k):
            if is_small(k):
                eng.wait_ge(parts_done, smalls(k))
            else:
                eng.wait_ge(e_lo_done, gathers(k))

        def pairs_ready(eng, k):
            for n, done in ((smalls(k), small_pair_done), (gathers(k), e_pair_done)):
                if n:
                    eng.wait_ge(done, n)

        def place_free(eng, k):
            if k >= K_RING:
                eng.wait_ge(u_done, slots_of_field(k - K_RING))
                if is_small(k - K_RING):
                    eng.wait_ge(small_pair_done, smalls(k - K_RING))

        def field_bank_read(eng, k):
            if is_small(k):
                parts_ready(eng, k)
            else:
                pairs_ready(eng, k)

        def slots_of_field(k):
            return LAST_TILE[max(k, 1)] // 2 + 1

        @block.sync
        def _(sp):
            sp.dma_start(ids_sb[:], ids).then_inc(ids_in, 16)

            def load(c):
                if c >= RAW_RING:
                    sp.wait_ge(hi_stacked, 2 * min(c - RAW_RING + 1, CHUNKS))
                    lo_ready(sp, c - RAW_RING)
                sp.dma_start(raw[:, c % RAW_RING, :], chunks[c]).then_inc(raw_in[c % RAW_RING], 16)

            def load_small(j):
                if j >= 2:
                    sp.wait_ge(onehot_done, VT * (j - 1))
                    sp.wait_ge(table_lo, j - 1)
                sp.dma_start(ids_all[j % 2], ids_row[j:j + 1, :].to_broadcast([VR, BATCH])).then_inc(small_in[j % 2], 16)
                sp.dma_start(table_raw[j % 2], tables[SMALL[j]].rearrange("(p c) x -> p c x", c=VT))\
                  .then_inc(small_in[j % 2], 16)

            sp.dma_start(row_no_sb[:], row_no).then_inc(row_no_in, 16)
            load_small(0)
            load(0)
            load_small(1)
            sp.dma_start(ident_sb[:], ident).then_inc(const_in, 16)
            sp.dma_start(sel_sb[:], sel).then_inc(const_in, 16)
            for c in range(1, RAW_RING):
                load(c)
            small = 2
            for c in range(CHUNKS):
                for _ in range(2):
                    if small < len(SMALL):
                        load_small(small)
                        small += 1
                lo_ready(sp, c)
                if c >= STACK_RING:
                    sp.wait_ge(u_done, (c - STACK_RING + 1) * CHUNK // 2)
                for half in range(2):
                    sp.dma_start(stack[P // 2 * (1 - half):P // 2 * (2 - half), c % STACK_RING, half, :].bitcast(f32),
                                 lo[P // 2 * half:P // 2 * (half + 1), c % LO_RING, :].bitcast(f32))\
                      .then_inc(lo_in[c % STACK_RING], 16)
                if c + RAW_RING < ALL_CHUNKS:
                    load(c + RAW_RING)
                if c == 8:
                    sp.dma_start(dsel_sb[:], dense_sel).then_inc(mlp_in, 16)
                    sp.dma_start(dense_sb[:], dense).then_inc(mlp_in, 16)
                    sp.dma_start(b1_sb[:], b1).then_inc(mlp_in, 16)
                    sp.dma_start(w2_sb[:], w2).then_inc(mlp_in, 16)
                    sp.dma_start(b2_sb[:], b2).then_inc(mlp_in, 16)
                    sp.dma_start(w3_sb[:], w3).then_inc(mlp_in, 16)
            for c in range(CHUNKS + RAW_RING, ALL_CHUNKS):
                load(c)
            sp.wait_ge(y_done, 1)
            sp.dma_start(out, y_sb).then_inc(stored, 16)
            sp.wait_ge(stored, 16)

        @block.gpsimd
        def _(pool):
            pool.wait_ge(ids_in, 16)
            for what, n in pool_order():
                if what == "gather":
                    g = gathers(n) - 1
                    if g >= G_RING:
                        pool.wait_ge(doubled, g - G_RING + 1)
                    for bt in range(BT):
                        pool.indirect_dma_start(
                            out=gathered[:, g % G_RING, bt, :], out_offset=None, in_=tables[ORDER[n]],
                            in_offset=bass.IndirectOffsetOnAxis(ap=ids_sb[:, bt, ORDER[n]:ORDER[n] + 1], axis=0))\
                            .then_inc(field_in[g % G_RING], 16)
                else:
                    pool.wait_ge(hi_done, n + 1)
                    if n < CHUNKS:
                        moved_out(pool, n)
                        lo_part, hi_part = lo[:, n % LO_RING, :], hi[:, n % HI_RING, :]
                    else:
                        lo_part, hi_part = stack[:, n % STACK_RING, 1, :], stack[:, n % STACK_RING, 0, :]
                    nc.gpsimd.tensor_tensor(lo_part, raw[:, n % RAW_RING, :], hi_part.bitcast(f32), ALU.subtract)\
                      .then_inc(lo_pool, 1)

        @block.scalar
        def _(act):
            def hi_parts(c):
                act.wait_ge(raw_in[c % RAW_RING], 16 * (c // RAW_RING + 1))
                if c < CHUNKS:
                    if c >= HI_RING:
                        lo_ready(act, c - HI_RING)
                    to = hi[:, c % HI_RING, :]
                else:
                    act.wait_ge(u_done, (c - STACK_RING + 1) * CHUNK // 2)
                    to = stack[:, c % STACK_RING, 0, :]
                nc.scalar.copy(to, raw[:, c % RAW_RING, :]).then_inc(hi_done, 1)

            def stack_hi(c, half):
                if c >= STACK_RING:
                    act.wait_ge(u_done, (c - STACK_RING + 1) * CHUNK // 2)
                rows = slice(P // 2 * half, P // 2 * (half + 1))
                nc.scalar.copy(stack[rows, c % STACK_RING, half, :], raw[rows, c % RAW_RING, :]).then_inc(hi_stacked, 1)

            for what, n in STEPS:
                if what == "O":
                    j = smalls(n) - 1
                    act.wait_ge(small_in[j % 2], 32 * (j // 2 + 1))
                    if j >= 2:
                        act.wait_ge(transposed, SMALL_AT[j - 2] + 1)
                    nc.scalar.copy(table_parts[j % 2][:, :, 0:EMB], table_raw[j % 2]).then_inc(table_hi, 1)
                elif what == "T" and is_small(n):
                    act.wait_ge(transposed, n + 1)
                    place_free(act, n)
                    for part, e_part in enumerate((e_hi, e_lo)):
                        for half in range(2):
                            last = nc.scalar.copy(e_part[EMB * half:EMB * (half + 1), n % K_RING, :],
                                                  psum[EMB * part:EMB * (part + 1), field_bank(n), :])
                    last.then_inc(parts_done, 1)
                elif what == "D":
                    g = gathers(n) - 1
                    act.wait_ge(field_in[g % G_RING], 16 * BT * (g // G_RING + 1))
                    if g >= D_RING:
                        act.wait_ge(transposed, GATHERED_AT[g - D_RING] + 1)
                    nc.scalar.copy(twice[:, g % D_RING, :, :, :], gathered[:, g % G_RING, :, :].rearrange(
                        "p t (o e) -> p t o e", o=1).to_broadcast([P, BT, 2, EMB])).then_inc(doubled, 1)
                elif what == "T":
                    act.wait_ge(transposed, n + 1)
                    place_free(act, n)
                    nc.scalar.copy(e_hi[:, n % K_RING, :], psum[:, field_bank(n), :]).then_inc(e_hi_done, 1)
                elif what == "P" and not is_small(n):
                    parts_ready(act, n)
                    rows = slice(EMB * (n % 2), EMB * (n % 2 + 1))
                    nc.scalar.copy(e_pairs[rows, n // 2, :], psum[rows, field_bank(n), :]).then_inc(e_pair_done, 1)
                elif what == "W":
                    hi_parts(n)
                elif what == "H":
                    stack_hi(n // 2, n % 2)
                elif what == "S" and block_ends(n):
                    act.wait_ge(reduced, n + 1 + (n == QUADS - 1))
                    nc.scalar.copy(z_hi[:, n // Z_WINDOWS, :], psum[:, Z_BANK, :]).then_inc(z_hi_done, 1)
            act.wait_ge(mlp_in, MLP_LOADS * 16)
            for n in range(0, H1 // P, 2):
                act.wait_ge(h1_mm, n + 1)
                nc.scalar.activation(h1_sb[:, n, :], psum[:, n, :], ACT.Relu, bias=b1_sb[:, n:n + 1])\
                  .then_inc(h1_act, 1)
            act.wait_ge(h2_mm, 1)
            nc.scalar.activation(h2_sb[:, 0, :], psum[:, 4, :], ACT.Relu, bias=b2_sb[:, 0:1]).then_inc(h2_act, 1)
            act.wait_ge(y_mm, 1)
            nc.scalar.copy(y_sb, psum[0:1, 6, :]).then_inc(y_done, 1)

        @block.vector
        def _(dve):
            for what, n in STEPS:
                if what == "L":
                    dve.wait_ge(hi_done, n + 1)
                    moved_out(dve, n)
                    nc.vector.tensor_tensor(lo[:, n % LO_RING, :], raw[:, n % RAW_RING, :],
                                            hi[:, n % HI_RING, :].bitcast(f32), ALU.subtract).then_inc(lo_dve, 1)
                elif what == "O":
                    j = smalls(n) - 1
                    dve.wait_ge(small_in[j % 2], 32 * (j // 2 + 1))
                    dve.wait_ge(row_no_in, 16)
                    dve.wait_ge(table_hi, j + 1)
                    nc.vector.tensor_tensor(table_parts[j % 2][:, :, EMB:2 * EMB], table_raw[j % 2],
                                            table_parts[j % 2][:, :, 0:EMB].bitcast(f32), ALU.subtract)\
                      .then_inc(table_lo, 1)
                    for i in range(VT * j, VT * (j + 1)):
                        if i >= 2 * ZB and (i == VT * j or (i - 2 * ZB) % VT == 0):
                            dve.wait_ge(transposed, SMALL_AT[(i - 2 * ZB) // VT] + 1)
                        nc.vector.tensor_scalar(onehot[:, i % (2 * ZB), :], ids_all[j % 2],
                                                row_no_sb[0:VR, i % VT:i % VT + 1], None, ALU.is_equal)\
                          .then_inc(onehot_done, 1)
                elif what == "P" and is_small(n):
                    parts_ready(dve, n)
                    rows = slice(EMB * (n % 2), EMB * (n % 2 + 1))
                    nc.vector.tensor_tensor(e_pairs[rows, n // 2, :], e_hi[rows, n % K_RING, :].bitcast(f32),
                                            e_lo[rows, n % K_RING, :].bitcast(f32), ALU.add).then_inc(small_pair_done, 1)
                elif what == "T" and not is_small(n):
                    dve.wait_ge(e_hi_done, gathers(n))
                    nc.vector.tensor_tensor(e_lo[:, n % K_RING, :], psum[:, field_bank(n), :],
                                            e_hi[:, n % K_RING, :].bitcast(f32), ALU.subtract)\
                      .then_inc(e_lo_done, 1)
                elif what == "M":
                    dve.wait_ge(u_done, n + 1)
                    pairs_ready(dve, TILES[2 * n + 1][0])
                    if n >= PROD_RING:
                        dve.wait_ge(reduced, (n - PROD_RING) // 2 + 1)
                    m = sorted((TILES[2 * n][1], TILES[2 * n + 1][1]))
                    if m[0] == m[1]:
                        e = e_pairs[:, m[0]:m[0] + 1, :].to_broadcast([P, 2, BATCH])
                    else:
                        e = e_pairs[:, m[0]:m[1] + 1, :]
                    u = slot_bank(n)
                    nc.vector.tensor_tensor(prod[:, n % PROD_RING, :, :], psum[:, u:u + 2, :], e, ALU.mult)\
                      .then_inc(prod_done, 1)
                elif what == "S" and block_ends(n):
                    b = n // Z_WINDOWS
                    dve.wait_ge(z_hi_done, b + 1)
                    nc.vector.tensor_tensor(z_lo[:, b, :], psum[:, Z_BANK, :], z_hi[:, b, :].bitcast(f32),
                                            ALU.subtract).then_inc(z_lo_done, 1)
            dve.wait_ge(mlp_in, MLP_LOADS * 16)
            for n in range(1, H1 // P, 2):
                dve.wait_ge(h1_mm, n + 1)
                nc.vector.tensor_scalar(h1_sb[:, n, :], psum[:, n, :], b1_sb[:, n:n + 1], 0.0, ALU.add, ALU.max)\
                  .then_inc(h1_dve, 1)
            dve.wait_ge(h2_mm, 2)
            nc.vector.tensor_scalar(h2_sb[:, 1, :], psum[:, 5, :], b2_sb[:, 1:2], 0.0, ALU.add, ALU.max)\
              .then_inc(h2_dve, 1)

        @block.tensor
        def _(pe):
            pe.wait_ge(const_in, 32)

            def transpose_field(k):
                before = last_with(field_bank, k, field_bank(k))
                if before is not None:
                    field_bank_read(pe, before)
                if is_small(k):
                    j = smalls(k) - 1
                    pe.wait_ge(table_lo, j + 1)
                    for c in range(VT):
                        i = VT * j + c
                        pe.wait_ge(onehot_done, i + 1)
                        last = nc.tensor.matmul(psum[:, field_bank(k), :], table_parts[j % 2][:, c, :],
                                                onehot[:, i % (2 * ZB), :], start=(c == 0), stop=(c == VT - 1))
                else:
                    g = gathers(k) - 1
                    pe.wait_ge(doubled, g + 1)
                    for bt in range(BT):
                        last = nc.tensor.transpose(psum[:, field_bank(k), P * bt:P * (bt + 1)],
                                                   twice[:, g % D_RING, bt, :, :].rearrange("p o e -> p (o e)"), ident_sb[:])
                last.then_inc(transposed, 1)

            def multiply_slot(s):
                before = last_with(slot_bank, s, slot_bank(s))
                if before is not None:
                    pe.wait_ge(prod_done, before + 1)
                elif slot_bank(s) == E_BANKS[1]:
                    field_bank_read(pe, last_with(field_bank, FIELDS, E_BANKS[1]))
                for t in (2 * s, 2 * s + 1):
                    k = TILES[t][0]
                    c, u = t // CHUNK, t % CHUNK // 2
                    if t % CHUNK == 0:
                        pe.wait_ge(hi_stacked, 2 * (c + 1))
                        pe.wait_ge(lo_in[c % STACK_RING], 32 * (c // STACK_RING + 1))
                    if t == FIRST_TILE[k]:
                        parts_ready(pe, k)
                    weights = stack[:, c % STACK_RING, t % 2, P * u:P * (u + 1)]
                    bank = psum[:, slot_bank(s) + place_in_slot(t), :]
                    nc.tensor.matmul(bank, weights, e_hi[:, k % K_RING, :], start=True, stop=False)
                    last = nc.tensor.matmul(bank, weights, e_lo[:, k % K_RING, :], start=False, stop=True)
                last.then_inc(u_done, 1)

            def reduce_quad(q):
                w = q % Z_WINDOWS
                pe.wait_ge(prod_done, 2 * q + 2)
                if q and w == 0:
                    pe.wait_ge(z_lo_done, q // Z_WINDOWS)
                last_window = Z_WINDOWS - 1 if q < QUADS - QUADS % Z_WINDOWS else QUADS % Z_WINDOWS - 1
                for g in range(4):
                    t = 4 * q + g
                    last = nc.tensor.matmul(psum[32 * g:32 * g + 32, Z_BANK, :], sel_sb[:, 30 - 2 * w:62 - 2 * w],
                                            prod[:, (t // 2) % PROD_RING, place_in_slot(t), :],
                                            start=(w == 0), stop=(w == last_window and (g > 0 or q < QUADS - 1)),
                                            skip_group_check=True)
                last.then_inc(reduced, 1)

            for what, n in STEPS:
                if what == "T":
                    transpose_field(n)
                elif what == "M":
                    multiply_slot(n)
                elif what == "S":
                    reduce_quad(n)
            pe.wait_ge(mlp_in, MLP_LOADS * 16)
            nc.tensor.matmul(psum[0:32, Z_BANK, :], dsel_sb[:], dense_sb[:], start=False, stop=True,
                             skip_group_check=True).then_inc(reduced, 1)

            pe.wait_ge(prod_done, SLOTS)
            for b in range(ZB):
                c = CHUNKS + b // 2
                pe.wait_ge(lo_pool, c + 1 - LO_ON_VECTOR)
                pe.wait_ge(z_lo_done, b + 1)
                for n in range(H1 // P):
                    at = H1 * (b % 2) + P * n
                    w_hi, w_lo = (stack[:, c % STACK_RING, part, at:at + P] for part in range(2))
                    nc.tensor.matmul(psum[:, n, :], w_hi, z_hi[:, b, :], start=(b == 0), stop=False)
                    nc.tensor.matmul(psum[:, n, :], w_hi, z_lo[:, b, :], start=False, stop=False)
                    mm = nc.tensor.matmul(psum[:, n, :], w_lo, z_hi[:, b, :], start=False, stop=(b == ZB - 1))
                    if b == ZB - 1:
                        mm.then_inc(h1_mm, 1)
            for c in range(H1 // P):
                pe.wait_ge(h1_dve if c % 2 else h1_act, c // 2 + 1)
                for n in range(H2 // P):
                    mm = nc.tensor.matmul(psum[:, 4 + n, :], w2_sb[:, c, P * n:P * (n + 1)], h1_sb[:, c, :],
                                          start=(c == 0), stop=(c == H1 // P - 1))
                    if c == H1 // P - 1:
                        mm.then_inc(h2_mm, 1)
            for c in range(H2 // P):
                pe.wait_ge(h2_dve if c else h2_act, 1)
                mm = nc.tensor.matmul(psum[0:1, 6, :], w3_sb[:, c, :], h2_sb[:, c, :],
                                      start=(c == 0), stop=(c == H2 // P - 1))
            mm.then_inc(y_mm, 1)


def kernel(**inputs):
    import concourse.bacc as bacc
    from concourse.bass_utils import run_bass_kernel_spmd

    x = {k: np.asarray(v) for k, v in inputs.items()}

    param = x["L0_rec_param"]
    swapped = param.transpose(2, 1, 0)
    pairs = np.full((NT, 2), PAIRS)
    weights = np.zeros((EMB, NT, 2, EMB), param.dtype)
    for t, (k, m) in enumerate(TILES):
        for h in range(2):
            if 2 * m + h < k:
                a, b = ORDER[2 * m + h], ORDER[k]
                pairs[t, h] = pair_index(min(a, b), max(a, b))
                weights[:, t, h, :] = (param if a < b else swapped)[:, pairs[t, h], :]
    param = weights.reshape(EMB, CHUNKS, CHUNK // 2, 2, P).transpose(1, 3, 0, 2, 4).reshape(CHUNKS, P, CHUNK // 2 * P)

    rows = np.full(ZB * P, PAIRS + DENSE)
    for t in range(NT):
        for h in range(2):
            if pairs[t, h] < PAIRS:
                rows[z_row(t, h)] = pairs[t, h]
    rows[(ZB - 1) * P + DENSE_ROW:(ZB - 1) * P + DENSE_ROW + DENSE] = PAIRS + np.arange(DENSE)
    w1 = x["W_top1"]
    w1 = np.concatenate([w1, np.zeros((1, H1), w1.dtype)])[np.append(rows, np.full((2 * W1_CHUNKS - ZB) * P, len(w1)))]
    w1 = w1.reshape(W1_CHUNKS, 2, P, H1).transpose(0, 2, 1, 3).reshape(W1_CHUNKS, P, 2 * H1)
    chunks = np.concatenate([param, w1])

    sel = np.zeros((P, 62), np.float32)
    sel[:EMB, 30] = 1
    sel[EMB:, 31] = 1
    dense_sel = np.zeros((DENSE, 32), np.float32)
    dense_sel[np.arange(DENSE), DENSE_ROW + np.arange(DENSE)] = 1

    arrays = {f"tbl{k}": x[f"tbl_{k}"] for k in range(FIELDS)}
    arrays |= {
        "idx": x["ids"].reshape(BT, P, FIELDS).transpose(1, 0, 2),
        "chunks": chunks, "row_no": np.arange(P * VT, dtype=np.float32).reshape(P, VT),
        "ids_row": x["ids"].T[list(SMALL)], "ident": np.eye(P, dtype=np.float32), "sel": sel, "dense_sel": dense_sel,
        "dense": x["dense_ctx"].T, "b1": x["b_top1"].reshape(H1 // P, P).T,
        "w2": x["W_top2"].reshape(H1 // P, P, H2).transpose(1, 0, 2), "b2": x["b_top2"].reshape(H2 // P, P).T,
        "w3": x["W_top3"].reshape(H2 // P, P, 1).transpose(1, 0, 2),
    }
    arrays = {f"in_{n}": np.ascontiguousarray(a) for n, a in arrays.items()}
    nc = bacc.Bacc("TRN2", target_bir_lowering=False, num_devices=1)
    ap = {n: nc.dram_tensor(n, a.shape, mybir.dt.from_np(a.dtype), kind="ExternalInput").ap() for n, a in arrays.items()}
    y = nc.dram_tensor("out_y", (1, BATCH), mybir.dt.float32, kind="ExternalOutput").ap()
    build(nc, [ap[f"in_tbl{k}"] for k in range(FIELDS)],
          *(ap[f"in_{n}"] for n in ("idx", "ids_row", "row_no", "chunks", "ident", "sel", "dense_sel", "dense", "b1", "w2", "b2", "w3")), y)
    result = run_bass_kernel_spmd(nc, [arrays], core_ids=[0])
    return result.results[0]["out_y"].reshape(BATCH, 1)
```

```python
import numpy as np
import concourse.bass as bass
from concourse import mybir

BATCH, FIELDS, EMB, DENSE = 512, 40, 64, 16
H1, H2 = 512, 256
P = 128
BT = BATCH // P
PAIRS = FIELDS * (FIELDS - 1) // 2

SMALL = (0, 6, 8)
VOCAB = 1000
VT = 8
VR = VOCAB // VT
ORDER = [*SMALL, *(f for f in range(FIELDS) if f not in SMALL)]


def is_small(k):
    return ORDER[k] in SMALL


def smalls(k):
    return sum(is_small(x) for x in range(k + 1))


def gathers(k):
    return k + 1 - smalls(k)


TILES = []
for _k in range(1, FIELDS):
    _ms = list(range((_k + 1) // 2))
    TILES += [(_k, m) for m in (_ms if _k % 2 else _ms[::-1])]
NT = len(TILES)
FIRST_TILE = {k: min(t for t, x in enumerate(TILES) if x[0] == k) for k in range(1, FIELDS)}
LAST_TILE = {k: max(t for t, x in enumerate(TILES) if x[0] == k) for k in range(1, FIELDS)}
SLOTS = NT // 2
QUADS = NT // 4
CHUNK = 16
CHUNKS = NT // CHUNK
ZT = 64
ZB = -(-NT // ZT)
W1_CHUNKS = -(-ZB // 2)
ALL_CHUNKS = CHUNKS + W1_CHUNKS
Z_WINDOWS = ZT // 4
DENSE_ROW = 2 * ((NT % ZT) // 4)


SMALL_AT = [k for k in range(FIELDS) if is_small(k)]
GATHERED_AT = [k for k in range(FIELDS) if not is_small(k)]


def pair_index(i, j):
    return i * (2 * FIELDS - i - 1) // 2 + j - i - 1


def z_row(t, half):
    return P * (t // ZT) + 32 * (t % 4) + 2 * ((t % ZT) // 4) + half


def place_in_slot(t):
    a, b = TILES[t - t % 2][1], TILES[t - t % 2 + 1][1]
    return t % 2 if a <= b else 1 - t % 2


Z_BANK, E_BANKS = 6, (7, 4)
EARLY_SLOTS, EARLY_FIELDS = 8, 9


def slot_bank(s):
    return 2 * (s % 2) if s < EARLY_SLOTS else 2 * (s % 3)


def field_bank(k):
    return E_BANKS[k % 2] if k < EARLY_FIELDS else E_BANKS[0]


def last_with(bank_of, n, bank):
    return max((x for x in range(n) if bank_of(x) == bank), default=None)


RAW_RING, HI_RING, LO_RING, STACK_RING = 3, 2, 2, 5
G_RING, D_RING, K_RING = 6, 3, 4
PROD_RING = 6
ONEHOT_AHEAD, DOUBLED_AHEAD = 1, 1
FIRST_CHUNKS = {0: 0, 1: 1, 2: 4, 3: 8}
AHEAD = 3
LO_ON_VECTOR = 4
LO_LATER, STACKED_LATER = 1, (1, 4)
POOL_LATER = 7
SINGLE_QUADS = 20
COUPLES = 18


def lead(k):
    return 1 if k < 6 else 4 if k < COUPLES else 9


def coupled(k):
    return k >= COUPLES


def arrivals(k):
    return sum(not is_small(x) for x in range(k % G_RING, k + 1, G_RING))


def schedule():
    steps, later = [], []

    def add(step, *followers):
        steps.append(step)
        if step[0] in "MT":
            for x in later:
                x[0] -= 1
            while any(x[0] <= 0 for x in later):
                x = next(x for x in later if x[0] <= 0)
                later.remove(x)
                steps.append(x[1])
        later.extend([n, x] for n, x in followers)

    def chunk(c):
        lo_part = [(LO_LATER, ("L", c))] if c < LO_ON_VECTOR else []
        halves = [(n, ("H", 2 * c + half)) for half, n in enumerate(STACKED_LATER)] if c < CHUNKS else []
        add(("W", c), *lo_part, *halves)

    k = quads = 0
    for s in range(SLOTS):
        while k < FIELDS and (k < 2 or 2 * s + 1 >= FIRST_TILE[k] - lead(k)):
            if coupled(k) and any(x[1][0] == "P" for x in later):
                break
            for x in range(len(SMALL)):
                if max(x - ONEHOT_AHEAD, 0) == k:
                    add(("O", x))
            for c, before in FIRST_CHUNKS.items():
                if before == k:
                    chunk(c)
            for x in range(FIELDS):
                if not is_small(x) and not coupled(x) and max(x - DOUBLED_AHEAD, 0) == k:
                    add(("D", x))
            add(("T", k), (1, ("P", k)))
            k += 2 if coupled(k) else 1
        if s and 2 * s % CHUNK == 0:
            chunk(2 * s // CHUNK + AHEAD)
        add(("M", s))
        while quads < QUADS and s >= (2 * quads + 3 if quads < SINGLE_QUADS else 2 * quads + 5):
            for _ in range(1 if quads < SINGLE_QUADS else 2):
                steps.append(("S", quads))
                quads += 1
    return steps + [("W", c) for c in range(CHUNKS + AHEAD, ALL_CHUNKS)] + [("S", q) for q in range(quads, QUADS)]


def pool_order():
    order, c = [], LO_ON_VECTOR
    for k in range(FIELDS):
        if not is_small(k):
            order.append(("gather", k))
        while c < CHUNKS and k >= TILES[CHUNK * (c - AHEAD)][0] + POOL_LATER:
            order.append(("lo", c))
            c += 1
    return order + [("lo", x) for x in range(c, ALL_CHUNKS)]


def build(nc, tables, ids, ids_row, row_no, chunks, ident, sel, dense_sel, dense, b1, w2, b2, w3, out):
    f32, f32r, i32 = mybir.dt.float32, mybir.dt.float32r, mybir.dt.int32
    ALU = mybir.AluOpType
    ACT = mybir.ActivationFunctionType
    STEPS = schedule()
    from contextlib import ExitStack
    ctx = ExitStack()
    with ctx:
        def sb(name, shape, dt=f32):
            return ctx.enter_context(nc.sbuf_tensor(name, shape, dt))

        def sem(name):
            return ctx.enter_context(nc.semaphore(name))

        row_no_sb = sb("row_no_sb", [P, VT])
        ids_sb = sb("ids_sb", [P, BT, FIELDS], i32)
        ident_sb = sb("ident_sb", [P, P])
        sel_sb = sb("sel_sb", [P, 62])
        dsel_sb = sb("dsel_sb", [DENSE, 32])
        dense_sb = sb("dense_sb", [DENSE, BATCH])
        gathered = sb("gathered", [P, G_RING // 2, BT, 2, EMB])
        twice = sb("twice", [P, D_RING, BT, 2, EMB])
        e_pairs = sb("e_pairs", [P, FIELDS // 2, BATCH])
        e_hi = sb("e_hi", [P, K_RING, BATCH], f32r)
        e_lo = sb("e_lo", [P, K_RING, BATCH], f32r)
        raw = sb("raw", [P, RAW_RING, CHUNK // 2 * P])
        hi = sb("hi", [P, HI_RING, CHUNK // 2 * P], f32r)
        lo = sb("lo", [P, LO_RING, CHUNK // 2 * P], f32r)
        stack = sb("stack", [P, STACK_RING, 2, CHUNK // 2 * P], f32r)
        prod = sb("prod", [P, PROD_RING, 2, BATCH])
        table_parts = [sb(f"table_parts{i}", [VR, VT, 2 * EMB], f32r) for i in range(2)]
        z_parts = sb("z_parts", [P, 2 * ZB, BATCH], f32r)
        z_hi, z_lo = z_parts[:, 0:ZB, :], z_parts[:, ZB:2 * ZB, :]
        w2_sb = sb("w2_sb", [P, H1 // P, H2])
        w3_sb = sb("w3_sb", [P, H2 // P, 1])
        b1_sb = sb("b1_sb", [P, H1 // P])
        b2_sb = sb("b2_sb", [P, H2 // P])
        h1_sb, h2_sb, y_sb = e_pairs[:, 0:4, :], e_pairs[:, 4:6, :], e_pairs[:, 6, 0:BT]
        onehot = z_parts[0:VR, :, :]
        ids_all = [e_pairs[0:VR, 16 + i, :].bitcast(i32) for i in range(2)]
        table_raw = [e_pairs[0:VR, 18 + i, :].rearrange("p (c x) -> p c x", x=EMB) for i in range(2)]

        psum = ctx.enter_context(nc.psum_tensor("psum", [P, 8, BATCH], f32))
        MLP_LOADS = 6

        ids_in, row_no_in, mlp_in = sem("ids_in"), sem("row_no_in"), sem("mlp_in")
        ident_in, sel_in = sem("ident_in"), sem("sel_in")
        raw_in = [sem(f"raw_in{i}") for i in range(RAW_RING)]
        lo_in = [sem(f"lo_in{i}") for i in range(STACK_RING)]
        field_in = [sem(f"field_in{i}") for i in range(G_RING)]
        hi_done = sem("hi_done")
        hi_stacked = [sem(f"hi_stacked{half}") for half in range(2)]
        lo_dve, lo_pool = sem("lo_dve"), sem("lo_pool")
        small_ids_in = [sem(f"small_ids_in{i}") for i in range(2)]
        small_in = [sem(f"small_in{i}") for i in range(2)]
        table_hi, table_lo = sem("table_hi"), sem("table_lo")
        onehot_done = sem("onehot_done")
        parts_done, small_pair_done = sem("parts_done"), sem("small_pair_done")
        doubled = sem("doubled")
        lo_doubled = sem("lo_doubled")
        transposed = sem("transposed")
        e_hi_done, e_pair_done = sem("e_hi_done"), sem("e_pair_done")
        e_lo_done = sem("e_lo_done")
        u_done = sem("u_done")
        prod_done = sem("prod_done")
        reduced = sem("reduced")
        z_hi_done, z_lo_done = sem("z_hi_done"), sem("z_lo_done")
        h1_mm, h1_act, h1_dve = sem("h1_mm"), sem("h1_act"), sem("h1_dve")
        h2_mm, h2_act, h2_dve = sem("h2_mm"), sem("h2_act"), sem("h2_dve")
        y_mm, y_done, stored = sem("y_mm"), sem("y_done"), sem("stored")
        block = ctx.enter_context(nc.Block())

        def rows_in(eng, k):
            eng.wait_ge(field_in[k % G_RING], 16 * BT * arrivals(k))

        def lo_ready(eng, c):
            if c < LO_ON_VECTOR:
                eng.wait_ge(lo_dve, c + 1)
            else:
                eng.wait_ge(lo_pool, c + 1 - LO_ON_VECTOR)

        def stacked(eng, c):
            for half in range(2):
                eng.wait_ge(hi_stacked[half], c + 1)

        def moved_out(eng, c):
            if c >= LO_RING:
                b = c - LO_RING
                eng.wait_ge(lo_in[b % STACK_RING], 32 * (b // STACK_RING + 1))

        def block_ends(q):
            return (q + 1) % Z_WINDOWS == 0 or q == QUADS - 1

        def parts_ready(eng, k):
            if is_small(k):
                eng.wait_ge(parts_done, smalls(k))
            elif coupled(k):
                eng.wait_ge(lo_doubled, k + 1 - COUPLES)
            else:
                eng.wait_ge(e_lo_done, gathers(k))

        def pairs_ready(eng, k):
            for n, done in ((smalls(k), small_pair_done), (gathers(k), e_pair_done)):
                if n:
                    eng.wait_ge(done, n)

        def place_free(eng, k):
            if k >= K_RING:
                eng.wait_ge(u_done, slots_of_field(k - K_RING))
                if is_small(k - K_RING):
                    eng.wait_ge(small_pair_done, smalls(k - K_RING))

        def field_bank_read(eng, k):
            if is_small(k):
                parts_ready(eng, k)
            else:
                pairs_ready(eng, k)

        def slots_of_field(k):
            return LAST_TILE[max(k, 1)] // 2 + 1

        @block.sync
        def _(sp):
            sp.dma_start(ids_sb[:], ids).then_inc(ids_in, 16)

            def load(c):
                if c >= RAW_RING:
                    stacked(sp, min(c - RAW_RING, CHUNKS - 1))
                    lo_ready(sp, c - RAW_RING)
                sp.dma_start(raw[:, c % RAW_RING, :], chunks[c]).then_inc(raw_in[c % RAW_RING], 16)

            def load_small(j):
                if j >= 2:
                    sp.wait_ge(onehot_done, VT * (j - 1))
                    sp.wait_ge(table_lo, j - 1)
                sp.dma_start(ids_all[j % 2], ids_row[j:j + 1, :].to_broadcast([VR, BATCH]))\
                  .then_inc(small_ids_in[j % 2], 16)
                sp.dma_start(table_raw[j % 2], tables[SMALL[j]].rearrange("(p c) x -> p c x", c=VT))\
                  .then_inc(small_in[j % 2], 16)

            sp.dma_start(row_no_sb[:], row_no).then_inc(row_no_in, 16)
            load_small(0)
            load(0)
            load_small(1)
            sp.dma_start(ident_sb[:], ident).then_inc(ident_in, 16)
            sp.dma_start(sel_sb[:], sel).then_inc(sel_in, 16)
            for c in range(1, RAW_RING):
                load(c)
            small = 2
            for c in range(CHUNKS):
                for _ in range(2):
                    if small < len(SMALL):
                        load_small(small)
                        small += 1
                lo_ready(sp, c)
                if c >= STACK_RING:
                    sp.wait_ge(u_done, (c - STACK_RING + 1) * CHUNK // 2)
                for half in range(2):
                    sp.dma_start(stack[P // 2 * (1 - half):P // 2 * (2 - half), c % STACK_RING, half, :].bitcast(f32),
                                 lo[P // 2 * half:P // 2 * (half + 1), c % LO_RING, :].bitcast(f32))\
                      .then_inc(lo_in[c % STACK_RING], 16)
                if c + RAW_RING < ALL_CHUNKS:
                    load(c + RAW_RING)
                if c == 8:
                    sp.dma_start(dsel_sb[:], dense_sel).then_inc(mlp_in, 16)
                    sp.dma_start(dense_sb[:], dense).then_inc(mlp_in, 16)
                    sp.dma_start(b1_sb[:], b1).then_inc(mlp_in, 16)
                    sp.dma_start(w2_sb[:], w2).then_inc(mlp_in, 16)
                    sp.dma_start(b2_sb[:], b2).then_inc(mlp_in, 16)
                    sp.dma_start(w3_sb[:], w3).then_inc(mlp_in, 16)
            for c in range(CHUNKS + RAW_RING, ALL_CHUNKS):
                load(c)
            sp.wait_ge(y_done, 1)
            sp.dma_start(out, y_sb).then_inc(stored, 16)
            sp.wait_ge(stored, 16)

        @block.gpsimd
        def _(pool):
            pool.wait_ge(ids_in, 16)
            for what, n in pool_order():
                if what == "gather":
                    before = n - G_RING
                    if before >= 0 and coupled(before):
                        pool.wait_ge(transposed, before + 1)
                    elif before >= 0 and not is_small(before):
                        pool.wait_ge(doubled, gathers(before))
                    for bt in range(BT):
                        pool.indirect_dma_start(
                            out=gathered[:, n % G_RING // 2, bt, n % 2, :], out_offset=None, in_=tables[ORDER[n]],
                            in_offset=bass.IndirectOffsetOnAxis(ap=ids_sb[:, bt, ORDER[n]:ORDER[n] + 1], axis=0))\
                            .then_inc(field_in[n % G_RING], 16)
                else:
                    pool.wait_ge(hi_done, n + 1)
                    if n < CHUNKS:
                        moved_out(pool, n)
                        lo_part, hi_part = lo[:, n % LO_RING, :], hi[:, n % HI_RING, :]
                    else:
                        lo_part, hi_part = stack[:, n % STACK_RING, 1, :], stack[:, n % STACK_RING, 0, :]
                    nc.gpsimd.tensor_tensor(lo_part, raw[:, n % RAW_RING, :], hi_part.bitcast(f32), ALU.subtract)\
                      .then_inc(lo_pool, 1)

        @block.scalar
        def _(act):
            def hi_parts(c):
                act.wait_ge(raw_in[c % RAW_RING], 16 * (c // RAW_RING + 1))
                if c < CHUNKS:
                    if c >= HI_RING:
                        lo_ready(act, c - HI_RING)
                    to = hi[:, c % HI_RING, :]
                else:
                    act.wait_ge(u_done, (c - STACK_RING + 1) * CHUNK // 2)
                    to = stack[:, c % STACK_RING, 0, :]
                nc.scalar.copy(to, raw[:, c % RAW_RING, :]).then_inc(hi_done, 1)

            def stack_hi(c, half):
                if c >= STACK_RING:
                    act.wait_ge(u_done, (c - STACK_RING + 1) * CHUNK // 2)
                rows = slice(P // 2 * half, P // 2 * (half + 1))
                nc.scalar.copy(stack[rows, c % STACK_RING, half, :], raw[rows, c % RAW_RING, :])\
                  .then_inc(hi_stacked[half], 1)

            for what, n in STEPS:
                if what == "O":
                    j = smalls(n) - 1
                    act.wait_ge(small_in[j % 2], 16 * (j // 2 + 1))
                    if j >= 2:
                        act.wait_ge(transposed, SMALL_AT[j - 2] + 1)
                    nc.scalar.copy(table_parts[j % 2][:, :, 0:EMB], table_raw[j % 2]).then_inc(table_hi, 1)
                elif what == "T" and is_small(n):
                    act.wait_ge(transposed, n + 1)
                    place_free(act, n)
                    for part, e_part in enumerate((e_hi, e_lo)):
                        for half in range(2):
                            last = nc.scalar.copy(e_part[EMB * half:EMB * (half + 1), n % K_RING, :],
                                                  psum[EMB * part:EMB * (part + 1), field_bank(n), :])
                    last.then_inc(parts_done, 1)
                elif what == "D":
                    g = gathers(n) - 1
                    rows_in(act, n)
                    if g >= D_RING:
                        act.wait_ge(transposed, GATHERED_AT[g - D_RING] + 1)
                    nc.scalar.copy(twice[:, g % D_RING, :, :, :], gathered[:, n % G_RING // 2, :, n % 2, :].rearrange(
                        "p t (o e) -> p t o e", o=1).to_broadcast([P, BT, 2, EMB])).then_inc(doubled, 1)
                elif what == "T" and coupled(n):
                    act.wait_ge(transposed, n + 2)
                    place_free(act, n + 1)
                    for k in (n, n + 1):
                        rows = slice(EMB * (k % 2), EMB * (k % 2 + 1))
                        nc.scalar.copy(e_hi[rows, k % K_RING, :], psum[rows, field_bank(n), :]).then_inc(e_hi_done, 1)
                    for k in (n, n + 1):
                        rows, others = (slice(EMB * h, EMB * (h + 1)) for h in (k % 2, 1 - k % 2))
                        act.wait_ge(e_hi_done, gathers(k))
                        nc.scalar.copy(e_hi[others, k % K_RING, :], e_hi[rows, k % K_RING, :])
                elif what == "P" and coupled(n):
                    for k in (n, n + 1):
                        rows, others = (slice(EMB * h, EMB * (h + 1)) for h in (k % 2, 1 - k % 2))
                        act.wait_ge(e_lo_done, gathers(k))
                        nc.scalar.copy(e_lo[others, k % K_RING, :], e_lo[rows, k % K_RING, :]).then_inc(lo_doubled, 1)
                    nc.scalar.copy(e_pairs[:, n // 2, :], psum[:, field_bank(n), :]).then_inc(e_pair_done, 2)
                elif what == "T":
                    act.wait_ge(transposed, n + 1)
                    place_free(act, n)
                    nc.scalar.copy(e_hi[:, n % K_RING, :], psum[:, field_bank(n), :]).then_inc(e_hi_done, 1)
                elif what == "P" and not is_small(n):
                    parts_ready(act, n)
                    rows = slice(EMB * (n % 2), EMB * (n % 2 + 1))
                    nc.scalar.copy(e_pairs[rows, n // 2, :], psum[rows, field_bank(n), :]).then_inc(e_pair_done, 1)
                elif what == "W":
                    hi_parts(n)
                elif what == "H":
                    stack_hi(n // 2, n % 2)
                elif what == "S" and block_ends(n):
                    act.wait_ge(reduced, n + 1 + (n == QUADS - 1))
                    nc.scalar.copy(z_hi[:, n // Z_WINDOWS, :], psum[:, Z_BANK, :]).then_inc(z_hi_done, 1)
            act.wait_ge(mlp_in, MLP_LOADS * 16)
            for n in range(0, H1 // P, 2):
                act.wait_ge(h1_mm, n + 1)
                nc.scalar.activation(h1_sb[:, n, :], psum[:, n, :], ACT.Relu, bias=b1_sb[:, n:n + 1])\
                  .then_inc(h1_act, 1)
            act.wait_ge(h2_mm, 1)
            nc.scalar.activation(h2_sb[:, 0, :], psum[:, 4, :], ACT.Relu, bias=b2_sb[:, 0:1]).then_inc(h2_act, 1)
            act.wait_ge(y_mm, 1)
            nc.scalar.copy(y_sb, psum[:, 0:BT, 0:1].rearrange("p t o -> p (t o)")).then_inc(y_done, 1)

        @block.vector
        def _(dve):
            for what, n in STEPS:
                if what == "L":
                    dve.wait_ge(hi_done, n + 1)
                    moved_out(dve, n)
                    nc.vector.tensor_tensor(lo[:, n % LO_RING, :], raw[:, n % RAW_RING, :],
                                            hi[:, n % HI_RING, :].bitcast(f32), ALU.subtract).then_inc(lo_dve, 1)
                elif what == "O":
                    j = smalls(n) - 1
                    dve.wait_ge(small_ids_in[j % 2], 16 * (j // 2 + 1))
                    dve.wait_ge(row_no_in, 16)
                    for i in range(VT * j, VT * (j + 1)):
                        if i >= 2 * ZB and (i == VT * j or (i - 2 * ZB) % VT == 0):
                            dve.wait_ge(transposed, SMALL_AT[(i - 2 * ZB) // VT] + 1)
                        nc.vector.tensor_scalar(onehot[:, i % (2 * ZB), :], ids_all[j % 2],
                                                row_no_sb[0:VR, i % VT:i % VT + 1], None, ALU.is_equal)\
                          .then_inc(onehot_done, 1)
                        if i == VT * j + 1:
                            dve.wait_ge(table_hi, j + 1)
                            nc.vector.tensor_tensor(table_parts[j % 2][:, :, EMB:2 * EMB], table_raw[j % 2],
                                                    table_parts[j % 2][:, :, 0:EMB].bitcast(f32), ALU.subtract)\
                              .then_inc(table_lo, 1)
                elif what == "P" and is_small(n):
                    parts_ready(dve, n)
                    rows = slice(EMB * (n % 2), EMB * (n % 2 + 1))
                    nc.vector.tensor_tensor(e_pairs[rows, n // 2, :], e_hi[rows, n % K_RING, :].bitcast(f32),
                                            e_lo[rows, n % K_RING, :].bitcast(f32), ALU.add).then_inc(small_pair_done, 1)
                elif what == "T" and coupled(n):
                    for k in (n, n + 1):
                        rows = slice(EMB * (k % 2), EMB * (k % 2 + 1))
                        dve.wait_ge(e_hi_done, gathers(n + 1))
                        nc.vector.tensor_tensor(e_lo[rows, k % K_RING, :], psum[rows, field_bank(n), :],
                                                e_hi[rows, k % K_RING, :].bitcast(f32), ALU.subtract)\
                          .then_inc(e_lo_done, 1)
                elif what == "T" and not is_small(n):
                    dve.wait_ge(e_hi_done, gathers(n))
                    nc.vector.tensor_tensor(e_lo[:, n % K_RING, :], psum[:, field_bank(n), :],
                                            e_hi[:, n % K_RING, :].bitcast(f32), ALU.subtract)\
                      .then_inc(e_lo_done, 1)
                elif what == "M":
                    dve.wait_ge(u_done, n + 1)
                    pairs_ready(dve, TILES[2 * n + 1][0])
                    if n >= PROD_RING:
                        dve.wait_ge(reduced, (n - PROD_RING) // 2 + 1)
                    m = sorted((TILES[2 * n][1], TILES[2 * n + 1][1]))
                    if m[0] == m[1]:
                        e = e_pairs[:, m[0]:m[0] + 1, :].to_broadcast([P, 2, BATCH])
                    else:
                        e = e_pairs[:, m[0]:m[1] + 1, :]
                    u = slot_bank(n)
                    nc.vector.tensor_tensor(prod[:, n % PROD_RING, :, :], psum[:, u:u + 2, :], e, ALU.mult)\
                      .then_inc(prod_done, 1)
                elif what == "S" and block_ends(n):
                    b = n // Z_WINDOWS
                    dve.wait_ge(z_hi_done, b + 1)
                    nc.vector.tensor_tensor(z_lo[:, b, :], psum[:, Z_BANK, :], z_hi[:, b, :].bitcast(f32),
                                            ALU.subtract).then_inc(z_lo_done, 1)
            dve.wait_ge(mlp_in, MLP_LOADS * 16)
            for n in range(1, H1 // P, 2):
                dve.wait_ge(h1_mm, n + 1)
                nc.vector.tensor_scalar(h1_sb[:, n, :], psum[:, n, :], b1_sb[:, n:n + 1], 0.0, ALU.add, ALU.max)\
                  .then_inc(h1_dve, 1)
            dve.wait_ge(h2_mm, 2)
            nc.vector.tensor_scalar(h2_sb[:, 1, :], psum[:, 5, :], b2_sb[:, 1:2], 0.0, ALU.add, ALU.max)\
              .then_inc(h2_dve, 1)

        @block.tensor
        def _(pe):
            def transpose_field(k):
                before = last_with(field_bank, k, field_bank(k))
                if before is not None:
                    field_bank_read(pe, before)
                if is_small(k):
                    j = smalls(k) - 1
                    pe.wait_ge(table_lo, j + 1)
                    for c in range(VT):
                        i = VT * j + c
                        pe.wait_ge(onehot_done, i + 1)
                        last = nc.tensor.matmul(psum[:, field_bank(k), :], table_parts[j % 2][:, c, :],
                                                onehot[:, i % (2 * ZB), :], start=(c == 0), stop=(c == VT - 1))
                elif coupled(k):
                    rows_in(pe, k)
                    rows_in(pe, k + 1)
                    for bt in range(BT):
                        last = nc.tensor.transpose(psum[:, field_bank(k), P * bt:P * (bt + 1)],
                                                   gathered[:, k % G_RING // 2, bt, :, :].rearrange("p o e -> p (o e)"),
                                                   ident_sb[:])
                else:
                    g = gathers(k) - 1
                    if g == 0:
                        pe.wait_ge(ident_in, 16)
                    pe.wait_ge(doubled, g + 1)
                    for bt in range(BT):
                        last = nc.tensor.transpose(psum[:, field_bank(k), P * bt:P * (bt + 1)],
                                                   twice[:, g % D_RING, bt, :, :].rearrange("p o e -> p (o e)"), ident_sb[:])
                last.then_inc(transposed, 2 if coupled(k) else 1)

            def multiply_slot(s):
                before = last_with(slot_bank, s, slot_bank(s))
                if before is not None:
                    pe.wait_ge(prod_done, before + 1)
                elif slot_bank(s) == E_BANKS[1]:
                    field_bank_read(pe, last_with(field_bank, FIELDS, E_BANKS[1]))
                for t in (2 * s, 2 * s + 1):
                    k = TILES[t][0]
                    c, u = t // CHUNK, t % CHUNK // 2
                    if t % CHUNK == 0:
                        stacked(pe, c)
                        pe.wait_ge(lo_in[c % STACK_RING], 32 * (c // STACK_RING + 1))
                    if t == FIRST_TILE[k]:
                        parts_ready(pe, k)
                    weights = stack[:, c % STACK_RING, t % 2, P * u:P * (u + 1)]
                    bank = psum[:, slot_bank(s) + place_in_slot(t), :]
                    nc.tensor.matmul(bank, weights, e_hi[:, k % K_RING, :], start=True, stop=False)
                    last = nc.tensor.matmul(bank, weights, e_lo[:, k % K_RING, :], start=False, stop=True)
                last.then_inc(u_done, 1)

            def reduce_quad(q):
                w = q % Z_WINDOWS
                if q == 0:
                    pe.wait_ge(sel_in, 16)
                pe.wait_ge(prod_done, 2 * q + 2)
                if q and w == 0:
                    pe.wait_ge(z_lo_done, q // Z_WINDOWS)
                last_window = Z_WINDOWS - 1 if q < QUADS - QUADS % Z_WINDOWS else QUADS % Z_WINDOWS - 1
                for g in range(4):
                    t = 4 * q + g
                    last = nc.tensor.matmul(psum[32 * g:32 * g + 32, Z_BANK, :], sel_sb[:, 30 - 2 * w:62 - 2 * w],
                                            prod[:, (t // 2) % PROD_RING, place_in_slot(t), :],
                                            start=(w == 0), stop=(w == last_window and (g > 0 or q < QUADS - 1)),
                                            skip_group_check=True)
                last.then_inc(reduced, 1)

            for what, n in STEPS:
                if what == "T":
                    transpose_field(n)
                elif what == "M":
                    multiply_slot(n)
                elif what == "S":
                    reduce_quad(n)
            pe.wait_ge(mlp_in, MLP_LOADS * 16)
            nc.tensor.matmul(psum[0:32, Z_BANK, :], dsel_sb[:], dense_sb[:], start=False, stop=True,
                             skip_group_check=True).then_inc(reduced, 1)

            pe.wait_ge(prod_done, SLOTS)
            for b in range(ZB):
                c = CHUNKS + b // 2
                pe.wait_ge(lo_pool, c + 1 - LO_ON_VECTOR)
                pe.wait_ge(z_lo_done, b + 1)
                for n in range(H1 // P):
                    at = H1 * (b % 2) + P * n
                    w_hi, w_lo = (stack[:, c % STACK_RING, part, at:at + P] for part in range(2))
                    nc.tensor.matmul(psum[:, n, :], w_hi, z_hi[:, b, :], start=(b == 0), stop=False)
                    nc.tensor.matmul(psum[:, n, :], w_hi, z_lo[:, b, :], start=False, stop=False)
                    mm = nc.tensor.matmul(psum[:, n, :], w_lo, z_hi[:, b, :], start=False, stop=(b == ZB - 1))
                    if b == ZB - 1:
                        mm.then_inc(h1_mm, 1)
            for c in range(H1 // P):
                pe.wait_ge(h1_dve if c % 2 else h1_act, c // 2 + 1)
                for n in range(H2 // P):
                    mm = nc.tensor.matmul(psum[:, 4 + n, :], w2_sb[:, c, P * n:P * (n + 1)], h1_sb[:, c, :],
                                          start=(c == 0), stop=(c == H1 // P - 1))
                    if c == H1 // P - 1:
                        mm.then_inc(h2_mm, 1)
            for c in range(H2 // P):
                pe.wait_ge(h2_dve if c else h2_act, 1)
                for bt in range(BT):
                    mm = nc.tensor.matmul(psum[:, bt, 0:1], h2_sb[:, c, P * bt:P * (bt + 1)], w3_sb[:, c, :],
                                          start=(c == 0), stop=(c == H2 // P - 1))
            mm.then_inc(y_mm, 1)


def kernel(**inputs):
    import concourse.bacc as bacc
    from concourse.bass_utils import run_bass_kernel_spmd

    x = {k: np.asarray(v) for k, v in inputs.items()}

    param = x["L0_rec_param"]
    swapped = param.transpose(2, 1, 0)
    pairs = np.full((NT, 2), PAIRS)
    weights = np.zeros((EMB, NT, 2, EMB), param.dtype)
    for t, (k, m) in enumerate(TILES):
        for h in range(2):
            if 2 * m + h < k:
                a, b = ORDER[2 * m + h], ORDER[k]
                pairs[t, h] = pair_index(min(a, b), max(a, b))
                weights[:, t, h, :] = (param if a < b else swapped)[:, pairs[t, h], :]
    param = weights.reshape(EMB, CHUNKS, CHUNK // 2, 2, P).transpose(1, 3, 0, 2, 4).reshape(CHUNKS, P, CHUNK // 2 * P)

    rows = np.full(ZB * P, PAIRS + DENSE)
    for t in range(NT):
        for h in range(2):
            if pairs[t, h] < PAIRS:
                rows[z_row(t, h)] = pairs[t, h]
    rows[(ZB - 1) * P + DENSE_ROW:(ZB - 1) * P + DENSE_ROW + DENSE] = PAIRS + np.arange(DENSE)
    w1 = x["W_top1"]
    w1 = np.concatenate([w1, np.zeros((1, H1), w1.dtype)])[np.append(rows, np.full((2 * W1_CHUNKS - ZB) * P, len(w1)))]
    w1 = w1.reshape(W1_CHUNKS, 2, P, H1).transpose(0, 2, 1, 3).reshape(W1_CHUNKS, P, 2 * H1)
    chunks = np.concatenate([param, w1])

    sel = np.zeros((P, 62), np.float32)
    sel[:EMB, 30] = 1
    sel[EMB:, 31] = 1
    dense_sel = np.zeros((DENSE, 32), np.float32)
    dense_sel[np.arange(DENSE), DENSE_ROW + np.arange(DENSE)] = 1

    arrays = {f"tbl{k}": x[f"tbl_{k}"] for k in range(FIELDS)}
    arrays |= {
        "idx": x["ids"].reshape(BT, P, FIELDS).transpose(1, 0, 2),
        "chunks": chunks, "row_no": np.arange(P * VT, dtype=np.float32).reshape(P, VT),
        "ids_row": x["ids"].T[list(SMALL)], "ident": np.eye(P, dtype=np.float32), "sel": sel, "dense_sel": dense_sel,
        "dense": x["dense_ctx"].T, "b1": x["b_top1"].reshape(H1 // P, P).T,
        "w2": x["W_top2"].reshape(H1 // P, P, H2).transpose(1, 0, 2), "b2": x["b_top2"].reshape(H2 // P, P).T,
        "w3": x["W_top3"].reshape(H2 // P, P, 1).transpose(1, 0, 2),
    }
    arrays = {f"in_{n}": np.ascontiguousarray(a) for n, a in arrays.items()}
    nc = bacc.Bacc("TRN2", target_bir_lowering=False, num_devices=1)
    ap = {n: nc.dram_tensor(n, a.shape, mybir.dt.from_np(a.dtype), kind="ExternalInput").ap() for n, a in arrays.items()}
    y = nc.dram_tensor("out_y", (P, BT), mybir.dt.float32, kind="ExternalOutput").ap()
    build(nc, [ap[f"in_tbl{k}"] for k in range(FIELDS)],
          *(ap[f"in_{n}"] for n in ("idx", "ids_row", "row_no", "chunks", "ident", "sel", "dense_sel", "dense", "b1", "w2", "b2", "w3")), y)
    result = run_bass_kernel_spmd(nc, [arrays], core_ids=[0])
    return result.results[0]["out_y"].T.reshape(BATCH, 1)
```
